# Optimizing a Trainium2 kernel written in Bass

```python
import numpy as np
import jax
import jax.numpy as jnp

def _softmax(x, axis=-1):
    return jax.nn.softmax(x, axis=axis)

def _gelu(x):
    return jax.nn.gelu(x, approximate=True)

def _silu(x):
    return jax.nn.silu(x)

def _sigmoid(x):
    return jax.nn.sigmoid(x)

def _layernorm(x, axis=-1, eps=1e-05):
    m = jnp.mean(x, axis=axis, keepdims=True)
    v = jnp.var(x, axis=axis, keepdims=True)
    return (x - m) / jnp.sqrt(v + eps)

def _scatter_add(tgt, idx, src, axis=0):
    return tgt.at[idx].add(src)

def _segment_sum(src, seg, n):
    return jax.ops.segment_sum(src, seg, n)
kernel_name = 'mk_hybrid_d2_jaxref_r8_fddde2'

def setup_inputs(seed: int=0):
    np.random.seed(seed)
    _w = jnp.asarray

    def _L0_attn_a_setup():
        import jax, jax.numpy as jnp
        import numpy as np
        DIM = 128
        HEADS = 16
        HEAD_DIM = DIM // HEADS
        ROPE_BASE = 500000.0
        SCALE = HEAD_DIM ** (-0.5)

        def _rope_cos_sin(T, dtype=jnp.float32):
            inv_freq = 1.0 / ROPE_BASE ** (jnp.arange(0, HEAD_DIM, 2, dtype=jnp.float32) / HEAD_DIM)
            t = jnp.arange(T, dtype=jnp.float32)
            freqs = t[:, None] * inv_freq[None, :]
            emb = jnp.concatenate([freqs, freqs], axis=-1)
            return (jnp.cos(emb).astype(dtype), jnp.sin(emb).astype(dtype))

        def _rotate_half(x):
            x1, x2 = jnp.split(x, 2, axis=-1)
            return jnp.concatenate([-x2, x1], axis=-1)

        def _apply_rope(x, cos, sin):
            return x * cos + _rotate_half(x) * sin
        key = jax.random.key(seed)
        k1, k2, k3 = jax.random.split(key, 3)
        B, T = (4, 512)
        x = jax.random.normal(k1, (B, T, DIM), dtype=jnp.float32)
        W_qkv = jax.random.normal(k2, (DIM, 3 * DIM), dtype=jnp.float32) * DIM ** (-0.5)
        W_out = jax.random.normal(k3, (DIM, DIM), dtype=jnp.float32) * DIM ** (-0.5)
        return {'x': x, 'W_qkv': W_qkv, 'W_out': W_out}
    _L0_attn_a_in = _L0_attn_a_setup()

    def _L0_attn_b_setup():
        import jax, jax.numpy as jnp
        import numpy as np
        D_MODEL, D_STATE, D_CONV, EXPAND = (128, 16, 4, 2)
        D_INNER = D_MODEL * EXPAND
        BATCH, T = (1, 256)
        key = jax.random.key(seed)
        ks = jax.random.split(key, 6)
        s = 0.02
        x = jax.random.normal(ks[0], (BATCH, T, D_MODEL), dtype=jnp.float32)
        W_in = jax.random.normal(ks[1], (2 * D_INNER, D_MODEL), dtype=jnp.float32) * s
        conv_w = jax.random.normal(ks[2], (D_INNER, 1, D_CONV), dtype=jnp.float32) * s
        conv_b = jnp.zeros((D_INNER,), dtype=jnp.float32)
        W_x = jax.random.normal(ks[3], (D_INNER + 2 * D_STATE, D_INNER), dtype=jnp.float32) * s
        A_log = jnp.log(jnp.arange(1, D_STATE + 1, dtype=jnp.float32))[None, :] * jnp.ones((D_INNER, 1), jnp.float32)
        D = jnp.ones((D_INNER,), dtype=jnp.float32)
        W_out = jax.random.normal(ks[4], (D_MODEL, D_INNER), dtype=jnp.float32) * s
        return {'x': x, 'W_in': W_in, 'conv_w': conv_w, 'conv_b': conv_b, 'W_x': W_x, 'A_log': A_log, 'D': D, 'W_out': W_out}
    _L0_attn_b_in = _L0_attn_b_setup()

    def _L0_ffn_setup():
        import jax, jax.numpy as jnp
        import numpy as np
        BLOCK = 16
        _GRID = jnp.array([0.0, 0.5, 1.0, 1.5, 2.0, 3.0, 4.0, 6.0], dtype=jnp.float32)
        _MID = jnp.array([0.25, 0.75, 1.25, 1.75, 2.5, 3.5, 5.0], dtype=jnp.float32)

        def fp4_quant_dequant(x):
            shape = x.shape
            xb = x.reshape(shape[:-1] + (shape[-1] // BLOCK, BLOCK))
            scale = jnp.max(jnp.abs(xb), axis=-1, keepdims=True) / 6.0
            scale = jnp.maximum(scale, jnp.float32(1e-12))
            xn = xb / scale
            idx = jnp.searchsorted(_MID, jnp.abs(xn))
            q = _GRID[idx] * jnp.sign(xn) * scale
            return q.reshape(shape)

        def fp4_linear(x, w):
            xq = fp4_quant_dequant(x)
            wq = fp4_quant_dequant(w)
            return jnp.einsum('bsk,nk->bsn', xq, wq)
        key = jax.random.key(seed)
        k1, k2, k3, k4 = jax.random.split(key, 4)
        H, I = (128, 352)
        x = jax.random.normal(k1, (4, 512, H), dtype=jnp.float32)
        w_gate = jax.random.normal(k2, (I, H), dtype=jnp.float32) * 0.02
        w_up = jax.random.normal(k3, (I, H), dtype=jnp.float32) * 0.02
        w_down = jax.random.normal(k4, (H, I), dtype=jnp.float32) * 0.02
        return {'x': x, 'w_gate': w_gate, 'w_up': w_up, 'w_down': w_down}
    _L0_ffn_in = _L0_ffn_setup()

    def _L1_attn_a_setup():
        import jax, jax.numpy as jnp
        import numpy as np
        import math
        D = 128
        H = 16
        HD = D // H
        NKV = H // 4
        SPARSE_K = 64
        TEMP = 1.0
        EPS = 1e-08

        def rmsnorm(x, w):
            return x * jax.lax.rsqrt(jnp.mean(x * x, axis=-1, keepdims=True) + EPS) * w

        def alibi_bias(n_head, T):
            slopes = 2.0 ** (-(jnp.arange(n_head, dtype=jnp.float32) / (n_head - 1) * 8.0))
            pos = jnp.arange(T)
            dist = jnp.abs(pos[:, None] - pos[None, :]).astype(jnp.float32)
            return -slopes[:, None, None] * dist[None, :, :]
        key = jax.random.key(seed)
        ks = jax.random.split(key, 8)
        B, T = (1, 256)
        s = 0.02
        return {'x': jax.random.normal(ks[0], (B, T, D), dtype=jnp.float32), 'wq': jax.random.normal(ks[1], (D, H * HD), dtype=jnp.float32) * s, 'bq': jnp.zeros((H * HD,), dtype=jnp.float32), 'wkv': jax.random.normal(ks[2], (D, 2 * NKV * HD), dtype=jnp.float32) * s, 'bkv': jnp.zeros((2 * NKV * HD,), dtype=jnp.float32), 'wo': jax.random.normal(ks[3], (H * HD, D), dtype=jnp.float32) * s, 'bo': jnp.zeros((D,), dtype=jnp.float32), 'qn_w': jnp.ones((HD,), dtype=jnp.float32), 'kn_w': jnp.ones((HD,), dtype=jnp.float32)}
    _L1_attn_a_in = _L1_attn_a_setup()

    def _L1_attn_b_setup():
        import jax, jax.numpy as jnp
        import numpy as np
        key = jax.random.key(seed)
        k1, k2, k3 = jax.random.split(key, 3)
        B, S, D, N = (2, 256, 128, 16)
        H = D // N
        x = jax.random.normal(k1, (B, S, D), dtype=jnp.float32)
        W_qkv = jax.random.normal(k2, (N, D, 3 * H), dtype=jnp.float32) / np.sqrt(D).astype(np.float32)
        W_out = jax.random.normal(k3, (N, H, D), dtype=jnp.float32) / np.sqrt(D).astype(np.float32)
        return {'x': x, 'W_qkv': W_qkv, 'W_out': W_out}
    _L1_attn_b_in = _L1_attn_b_setup()

    def _L1_ffn_setup():
        import jax, jax.numpy as jnp
        import numpy as np
        D_MODEL, D_FF, RANK = (128, 512, 32)
        B, S = (4, 512)
        key = jax.random.key(seed)
        ks = jax.random.split(key, 7)
        return {'x': jax.random.normal(ks[0], (B, S, D_MODEL), dtype=jnp.float32), 'U1': jax.random.normal(ks[1], (D_MODEL, RANK), dtype=jnp.float32) * 0.02, 'V1': jax.random.normal(ks[2], (RANK, D_FF), dtype=jnp.float32) * 0.02, 'b1': jnp.zeros((D_FF,), dtype=jnp.float32), 'U2': jax.random.normal(ks[3], (D_FF, RANK), dtype=jnp.float32) * 0.02, 'V2': jax.random.normal(ks[4], (RANK, D_MODEL), dtype=jnp.float32) * 0.02, 'b2': jnp.zeros((D_MODEL,), dtype=jnp.float32)}
    _L1_ffn_in = _L1_ffn_setup()
    _d = {'L0_attn_a_x': _L0_attn_a_in['x'], 'L0_attn_a_W_qkv': _L0_attn_a_in['W_qkv'], 'L0_attn_a_W_out': _L0_attn_a_in['W_out'], 'L0_attn_b_W_in': _L0_attn_b_in['W_in'], 'L0_attn_b_conv_w': _L0_attn_b_in['conv_w'], 'L0_attn_b_conv_b': _L0_attn_b_in['conv_b'], 'L0_attn_b_W_x': _L0_attn_b_in['W_x'], 'L0_attn_b_A_log': _L0_attn_b_in['A_log'], 'L0_attn_b_D': _L0_attn_b_in['D'], 'L0_attn_b_W_out': _L0_attn_b_in['W_out'], 'L0_ffn_w_gate': _L0_ffn_in['w_gate'], 'L0_ffn_w_up': _L0_ffn_in['w_up'], 'L0_ffn_w_down': _L0_ffn_in['w_down'], 'L1_attn_a_wq': _L1_attn_a_in['wq'], 'L1_attn_a_bq': _L1_attn_a_in['bq'], 'L1_attn_a_wkv': _L1_attn_a_in['wkv'], 'L1_attn_a_bkv': _L1_attn_a_in['bkv'], 'L1_attn_a_wo': _L1_attn_a_in['wo'], 'L1_attn_a_bo': _L1_attn_a_in['bo'], 'L1_attn_a_qn_w': _L1_attn_a_in['qn_w'], 'L1_attn_a_kn_w': _L1_attn_a_in['kn_w'], 'L1_attn_b_W_qkv': _L1_attn_b_in['W_qkv'], 'L1_attn_b_W_out': _L1_attn_b_in['W_out'], 'L1_ffn_U1': _L1_ffn_in['U1'], 'L1_ffn_V1': _L1_ffn_in['V1'], 'L1_ffn_b1': _L1_ffn_in['b1'], 'L1_ffn_U2': _L1_ffn_in['U2'], 'L1_ffn_V2': _L1_ffn_in['V2'], 'L1_ffn_b2': _L1_ffn_in['b2']}
    _x0 = _d['L0_attn_a_x']
    _d['L0_attn_a_x'] = jax.random.normal(jax.random.fold_in(jax.random.key(seed), 1), (4, 1024, 128), dtype=_x0.dtype)
    del _x0
    return _d

def reference(L0_attn_a_x, L0_attn_a_W_qkv, L0_attn_a_W_out, L0_attn_b_W_in, L0_attn_b_conv_w, L0_attn_b_conv_b, L0_attn_b_W_x, L0_attn_b_A_log, L0_attn_b_D, L0_attn_b_W_out, L0_ffn_w_gate, L0_ffn_w_up, L0_ffn_w_down, L1_attn_a_wq, L1_attn_a_bq, L1_attn_a_wkv, L1_attn_a_bkv, L1_attn_a_wo, L1_attn_a_bo, L1_attn_a_qn_w, L1_attn_a_kn_w, L1_attn_b_W_qkv, L1_attn_b_W_out, L1_ffn_U1, L1_ffn_V1, L1_ffn_b1, L1_ffn_U2, L1_ffn_V2, L1_ffn_b2):

    def _L0_attn_a_ref(x, W_qkv, W_out):
        import jax, jax.numpy as jnp
        import numpy as np
        DIM = 128
        HEADS = 16
        HEAD_DIM = DIM // HEADS
        ROPE_BASE = 500000.0
        SCALE = HEAD_DIM ** (-0.5)

        def _rope_cos_sin(T, dtype=jnp.float32):
            inv_freq = 1.0 / ROPE_BASE ** (jnp.arange(0, HEAD_DIM, 2, dtype=jnp.float32) / HEAD_DIM)
            t = jnp.arange(T, dtype=jnp.float32)
            freqs = t[:, None] * inv_freq[None, :]
            emb = jnp.concatenate([freqs, freqs], axis=-1)
            return (jnp.cos(emb).astype(dtype), jnp.sin(emb).astype(dtype))

        def _rotate_half(x):
            x1, x2 = jnp.split(x, 2, axis=-1)
            return jnp.concatenate([-x2, x1], axis=-1)

        def _apply_rope(x, cos, sin):
            return x * cos + _rotate_half(x) * sin
        B, T, D = x.shape
        H, hd = (HEADS, HEAD_DIM)
        qkv = (x @ W_qkv).reshape(B, T, 3, H, hd).transpose(2, 0, 3, 1, 4)
        q, k, v = (qkv[0], qkv[1], qkv[2])
        cos, sin = _rope_cos_sin(T, q.dtype)
        q = _apply_rope(q, cos, sin)
        k = _apply_rope(k, cos, sin)
        q_feat = jax.nn.elu(q * SCALE) + 1.0
        k_feat = jax.nn.elu(k) + 1.0
        kv = jnp.einsum('bhtd,bhtv->bhdv', k_feat, v)
        k_sum = k_feat.sum(axis=2)
        denom = jnp.maximum(jnp.einsum('bhtd,bhd->bht', q_feat, k_sum), 1e-06)
        out = jnp.einsum('bhtd,bhdv->bhtv', q_feat, kv) / denom[..., None]
        out = out.transpose(0, 2, 1, 3).reshape(B, T, D)
        return out @ W_out

    def _L0_attn_b_ref(x, W_in, conv_w, conv_b, W_x, A_log, D, W_out):
        import jax, jax.numpy as jnp
        import numpy as np
        D_MODEL, D_STATE, D_CONV, EXPAND = (128, 16, 4, 2)
        D_INNER = D_MODEL * EXPAND
        BATCH, T = (1, 256)
        B, Tlen, _ = x.shape
        E = D.shape[0]
        N = A_log.shape[1]
        K = conv_w.shape[-1]
        xz = x @ W_in.T
        x_in, z = (xz[..., :E], xz[..., E:])
        h = jax.lax.conv_general_dilated(x_in.transpose(0, 2, 1), conv_w, (1,), [(K - 1, 0)], dimension_numbers=('NCH', 'OIH', 'NCH'), feature_group_count=E)
        h = h + conv_b[None, :, None]
        h_conv = jax.nn.silu(h).transpose(0, 2, 1)
        dBC = h_conv @ W_x.T
        delta = jax.nn.softplus(dBC[..., :E])
        B_ssm = dBC[..., E:E + N]
        C_ssm = dBC[..., E + N:]
        A = -jnp.exp(A_log)
        A_bar = jnp.exp(delta[..., None] * A)
        Bu = delta[..., None] * B_ssm[:, :, None, :] * h_conv[..., None]

        def comb(l, r):
            a1, b1 = l
            a2, b2 = r
            return (a2 * a1, a2 * b1 + b2)
        _, hstates = jax.lax.associative_scan(comb, (A_bar, Bu), axis=1)
        y = jnp.einsum('bten,btn->bte', hstates, C_ssm) + h_conv * D
        y = y * jax.nn.silu(z)
        return y @ W_out.T

    def _L0_ffn_ref(x, w_gate, w_up, w_down):
        import jax, jax.numpy as jnp
        import numpy as np
        BLOCK = 16
        _GRID = jnp.array([0.0, 0.5, 1.0, 1.5, 2.0, 3.0, 4.0, 6.0], dtype=jnp.float32)
        _MID = jnp.array([0.25, 0.75, 1.25, 1.75, 2.5, 3.5, 5.0], dtype=jnp.float32)

        def fp4_quant_dequant(x):
            shape = x.shape
            xb = x.reshape(shape[:-1] + (shape[-1] // BLOCK, BLOCK))
            scale = jnp.max(jnp.abs(xb), axis=-1, keepdims=True) / 6.0
            scale = jnp.maximum(scale, jnp.float32(1e-12))
            xn = xb / scale
            idx = jnp.searchsorted(_MID, jnp.abs(xn))
            q = _GRID[idx] * jnp.sign(xn) * scale
            return q.reshape(shape)

        def fp4_linear(x, w):
            xq = fp4_quant_dequant(x)
            wq = fp4_quant_dequant(w)
            return jnp.einsum('bsk,nk->bsn', xq, wq)
        gate = fp4_linear(x, w_gate)
        y = fp4_linear(x, w_up)
        h = jax.nn.silu(gate) * y
        return fp4_linear(h, w_down)

    def _L1_attn_a_ref(x, wq, bq, wkv, bkv, wo, bo, qn_w, kn_w):
        import jax, jax.numpy as jnp
        import numpy as np
        import math
        D = 128
        H = 16
        HD = D // H
        NKV = H // 4
        SPARSE_K = 64
        TEMP = 1.0
        EPS = 1e-08

        def rmsnorm(x, w):
            return x * jax.lax.rsqrt(jnp.mean(x * x, axis=-1, keepdims=True) + EPS) * w

        def alibi_bias(n_head, T):
            slopes = 2.0 ** (-(jnp.arange(n_head, dtype=jnp.float32) / (n_head - 1) * 8.0))
            pos = jnp.arange(T)
            dist = jnp.abs(pos[:, None] - pos[None, :]).astype(jnp.float32)
            return -slopes[:, None, None] * dist[None, :, :]
        B, T, C = x.shape
        scale = 1.0 / math.sqrt(HD)
        q = (x @ wq + bq).reshape(B, T, H, HD).transpose(0, 2, 1, 3)
        kv = (x @ wkv + bkv).reshape(B, T, 2, NKV, HD)
        k = kv[:, :, 0].transpose(0, 2, 1, 3)
        v = kv[:, :, 1].transpose(0, 2, 1, 3)
        q = rmsnorm(q, qn_w)
        k = rmsnorm(k, kn_w)
        rep = H // NKV
        k = jnp.repeat(k, rep, axis=1)
        v = jnp.repeat(v, rep, axis=1)
        bias = alibi_bias(H, T)
        causal = jnp.triu(jnp.ones((T, T), dtype=bool), 1)
        pre = jnp.einsum('bhqd,bhkd->bhqk', q, k) * scale + bias[None]
        pre = jnp.where(causal, -jnp.inf, pre)
        kk = min(SPARSE_K, T)
        _, topk_idx = jax.lax.top_k(pre, kk)
        bi = jnp.arange(B)[:, None, None, None]
        hi = jnp.arange(H)[None, :, None, None]
        ti = jnp.arange(T)[None, None, :, None]
        sparse_mask = jnp.zeros((B, H, T, T), dtype=bool).at[bi, hi, ti, topk_idx].set(True)
        att = jnp.einsum('bhqd,bhkd->bhqk', q, k) * scale + bias[None]
        att = jnp.where(causal[None, None] | ~sparse_mask, -jnp.inf, att)
        att = jax.nn.softmax(att, axis=-1)
        y = jnp.einsum('bhqk,bhkd->bhqd', att, v)
        y = y.transpose(0, 2, 1, 3).reshape(B, T, C)
        return y @ wo + bo

    def _L1_attn_b_ref(x, W_qkv, W_out):
        import jax, jax.numpy as jnp
        import numpy as np
        B, S, D = x.shape
        head_dim = W_qkv.shape[-1] // 3
        qkv = jnp.einsum('bsd,ndh->bnsh', x, W_qkv)
        q, k, v = jnp.split(qkv, 3, axis=-1)
        scale = jnp.asarray(1.0 / np.sqrt(head_dim), dtype=x.dtype)
        attn = jnp.einsum('bnqh,bnkh->bnqk', q, k) * scale
        mask = jnp.asarray(-10000000000.0, dtype=x.dtype) * (1.0 - jnp.tril(jnp.ones((S, S), dtype=x.dtype)))
        attn = jax.nn.softmax(attn + mask, axis=-1)
        out = jnp.einsum('bnqk,bnkh->bnqh', attn, v)
        out = out.reshape(B, -1, S)
        return jnp.einsum('bds,nhd->bsd', out, W_out)

    def _L1_ffn_ref(x, U1, V1, b1, U2, V2, b2):
        import jax, jax.numpy as jnp
        import numpy as np
        D_MODEL, D_FF, RANK = (128, 512, 32)
        B, S = (4, 512)
        P = jnp.einsum('bsd,dr->bsr', x, U1)
        H = jax.nn.gelu(jnp.einsum('bsr,rf->bsf', P, V1) + b1)
        Q = jnp.einsum('bsf,fr->bsr', H, U2)
        return jnp.einsum('bsr,rd->bsd', Q, V2) + b2
    x = L0_attn_a_x
    x = x + _L0_attn_a_ref(_layernorm(x, axis=-1), L0_attn_a_W_qkv, L0_attn_a_W_out)
    x = x + _L0_ffn_ref(_layernorm(x, axis=-1), L0_ffn_w_gate, L0_ffn_w_up, L0_ffn_w_down)
    x = x + _L0_attn_b_ref(_layernorm(x, axis=-1), L0_attn_b_W_in, L0_attn_b_conv_w, L0_attn_b_conv_b, L0_attn_b_W_x, L0_attn_b_A_log, L0_attn_b_D, L0_attn_b_W_out)
    x = x + _L0_ffn_ref(_layernorm(x, axis=-1), L0_ffn_w_gate, L0_ffn_w_up, L0_ffn_w_down)
    x = x + _L1_attn_a_ref(_layernorm(x, axis=-1), L1_attn_a_wq, L1_attn_a_bq, L1_attn_a_wkv, L1_attn_a_bkv, L1_attn_a_wo, L1_attn_a_bo, L1_attn_a_qn_w, L1_attn_a_kn_w)
    x = x + _L1_ffn_ref(_layernorm(x, axis=-1), L1_ffn_U1, L1_ffn_V1, L1_ffn_b1, L1_ffn_U2, L1_ffn_V2, L1_ffn_b2)
    x = x + _L1_attn_b_ref(_layernorm(x, axis=-1), L1_attn_b_W_qkv, L1_attn_b_W_out)
    x = x + _L1_ffn_ref(_layernorm(x, axis=-1), L1_ffn_U1, L1_ffn_V1, L1_ffn_b1, L1_ffn_U2, L1_ffn_V2, L1_ffn_b2)
    return x

_drawn_inputs = setup_inputs


def setup_inputs(seed=0):
    import zlib

    import numpy as np

    out = dict(_drawn_inputs(seed))
    spreads = {'L0_attn_b_conv_b': (0.0, 0.8),
     'L0_attn_b_D': (1.0, 0.6),
     'L1_attn_a_bq': (0.0, 2.0),
     'L1_attn_a_bkv': (0.0, 2.0),
     'L1_attn_a_bo': (0.0, 0.8),
     'L1_attn_a_qn_w': (1.0, 0.6),
     'L1_attn_a_kn_w': (1.0, 0.6),
     'L1_ffn_b1': (0.0, 0.8),
     'L1_ffn_b2': (0.0, 0.8)}
    factors = {'L0_attn_b_W_in': 8.0,
     'L0_attn_b_conv_w': 8.0,
     'L0_attn_b_W_x': 8.0,
     'L0_attn_b_A_log': 8.0,
     'L0_attn_b_W_out': 8.0,
     'L0_ffn_w_gate': 2.913,
     'L0_ffn_w_up': 2.83,
     'L0_ffn_w_down': 2.843,
     'L1_attn_a_wq': 41.04,
     'L1_attn_a_wkv': 23.856,
     'L1_ffn_U1': 8.0,
     'L1_ffn_V1': 8.0,
     'L1_ffn_U2': 8.0,
     'L1_ffn_V2': 8.0,
     'L1_attn_a_wo': 8.0,
     'L1_attn_b_W_qkv': 4.797,
     'L1_attn_b_W_out': 4.912}
    for name, (base, spread) in spreads.items():
        noise = np.random.default_rng([zlib.crc32(name.encode()), seed]).standard_normal(out[name].shape)
        drawn = base * np.exp(spread * noise) if base else spread * noise
        out[name] = jnp.asarray(drawn.astype(out[name].dtype))
    for name, factor in factors.items():
        out[name] = (out[name] * factor).astype(out[name].dtype)
    return out
```

```python
from contextlib import ExitStack

import numpy as np

import concourse.bass as bass
from concourse import mybir

F32 = mybir.dt.float32
BF16 = mybir.dt.bfloat16
ALU = mybir.AluOpType
ACT = mybir.ActivationFunctionType
AX = mybir.AxisListType

B, T, D = 4, 1024, 128
P = 128
J = T // P
H, HD = 16, 8
NKV = 4
TOPK = 64
SCALE = HD ** -0.5
LN_EPS, RMS_EPS = 1e-5, 1e-8
FF4 = 352
FP4_BLOCK = 16
E_IN, NS, KCONV = 256, 16, 4
RANK, FFL = 32, 512
NEG = -1e30
BANK = 512
KSPLIT = 9 * HD
KBIAS = 9


class Chain:

    def __init__(self, eng, sem):
        self.eng, self.sem, self.n = eng, sem, 0

    def restart(self):
        self.eng.sem_clear(self.sem)
        self.n = 0

    def __call__(self, instruction):
        self.n += 1
        instruction.then_inc(self.sem, 1)
        self.eng.wait_ge(self.sem, self.n)

    def settled(self):
        self.eng.wait_ge(self.sem, self.n)


def rows_of(x, b):
    return x[:, bass.ds(b * T, T)]


def jd(ap):
    return ap.rearrange("p (j d) -> p j d", d=D)


def by_token(ap):
    return ap.rearrange("f (p j) -> f j p", j=J)


def along(ap, n):
    return ap.unsqueeze(2).broadcast_to([ap.shape[0], ap.shape[1], n])


def middle(ap, n):
    return ap.unsqueeze(1).broadcast_to([ap.shape[0], n, ap.shape[1]])


class Norm:

    def __init__(self, k, ps):
        self.k, self.nc, self.ps = k, k.nc, ps
        self.xc = k.sb("xc", [P, J * D])
        self.sq = k.sb("sq", [P, J * D])
        self.xn = k.sb("xn", [P, J * D])
        self.xT = k.sb("xT", [D, T])
        self.mean = k.sb("mean", [P, J])
        self.var = k.sb("var", [P, J])
        self.vare = k.sb("vare", [P, J])
        self.rstd = k.sb("rstd", [P, J])
        self.var_ready = k.sem("var_ready")
        self.rstd_ready = k.sem("rstd_ready")
        self.xn_ready = k.sem("xn_ready")
        self.xT_in_psum = k.sem("xT_in_psum")
        self.xT_ready = k.sem("xT_ready")

    def vector(self, dve, link, b, x, xn_used=None):
        v = self.nc.vector
        link(v.tensor_reduce(self.mean[:], jd(rows_of(x, b)), AX.X, ALU.add))
        link(v.tensor_scalar(self.mean[:], self.mean[:], 1.0 / D, None, ALU.mult))
        link(v.tensor_tensor(jd(self.xc[:]), jd(rows_of(x, b)), along(self.mean[:], D), ALU.subtract))
        link(v.tensor_tensor(self.sq[:], self.xc[:], self.xc[:], ALU.mult))
        link(v.tensor_reduce(self.var[:], jd(self.sq[:]), AX.X, ALU.add))
        v.tensor_scalar(self.vare[:], self.var[:], 1.0 / D, LN_EPS, ALU.mult, ALU.add).then_inc(self.var_ready, 1)
        dve.wait_ge(self.rstd_ready, b + 1)
        if xn_used is not None:
            dve.wait_ge(xn_used, b)
        v.tensor_tensor(jd(self.xn[:]), jd(self.xc[:]), along(self.rstd[:], D), ALU.mult).then_inc(self.xn_ready, 1)

    def pool(self, pool, b):
        pool.wait_ge(self.var_ready, b + 1)
        self.nc.gpsimd.tensor_tensor(self.rstd[:], self.vare[:], self.k.minus_half[:, 0:J], ALU.pow).then_inc(self.rstd_ready, 1)

    def tensor(self, pe, b):
        pe.wait_ge(self.xn_ready, b + 1)
        for j in range(J):
            last = self.nc.tensor.transpose(self.ps[:, j * P:(j + 1) * P], self.xn[:, j * D:(j + 1) * D], self.k.ident[:])
        last.then_inc(self.xT_in_psum, 1)

    def scalar(self, act, b, xT_used):
        act.wait_ge(self.xT_in_psum, b + 1)
        act.wait_ge(xT_used, b)
        for h in range(2):
            last = self.nc.scalar.copy(by_token(self.xT[:])[:, 4 * h:4 * h + 4, :],
                                       self.ps[:, h * BANK:(h + 1) * BANK].rearrange("d (j p) -> d j p", p=P))
        last.then_inc(self.xT_ready, 1)


class Kernel:
    def __init__(self, nc, dram, ctx):
        self.nc, self.dram, self.ctx, self.n, self.sems = nc, dram, ctx, 0, []

    def sb(self, name, shape, dt=F32):
        self.n += 1
        return self.ctx.enter_context(self.nc.sbuf_tensor(f"{name}_{self.n}", shape, dt))

    def sem(self, name):
        self.n += 1
        self.sems.append(self.nc.alloc_semaphore(f"{name}_{self.n}"))
        return self.sems[-1]

    def end_stage(self):
        self.nc.clear_and_free_semaphores(self.sems)
        self.sems = []
        self.nc.all_engine_barrier()


def load(nc, k, x, stage_loads):
    loaded, halves = k.sem("loaded"), k.sem("halves")
    with nc.Block() as block:
        @block.sync
        def _(sp):
            sp.dma_start(x[:].rearrange("p (b n) -> p b n", b=B),
                         k.dram["x"].rearrange("b (p j) d -> p b (j d)", j=J)).then_inc(loaded, 16)
            for to, of in stage_loads:
                sp.dma_start(to, of).then_inc(loaded, 16)
            sp.wait_ge(loaded, 16 * (1 + len(stage_loads)))

        @block.gpsimd
        def _(pool):
            nc.gpsimd.memset(k.minus_half[:], -0.5).then_inc(halves, 1)
            nc.gpsimd.memset(k.zeros[:], 0.0).then_inc(halves, 1)
            pool.wait_ge(halves, 2)


def store(nc, k, x, out):
    stored = k.sem("stored")
    with nc.Block() as block:
        @block.sync
        def _(sp):
            sp.dma_start(out.rearrange("b (p j) d -> p b (j d)", j=J),
                         x[:].rearrange("p (b n) -> p b n", b=B)).then_inc(stored, 16)
            sp.wait_ge(stored, 16)


def linear_attention(nc, k, x):
    dram = k.dram
    ps = k.ps
    norm = Norm(k, ps[:, 0:2 * BANK])
    wq = k.sb("wq", [D, 2 * D])
    wkv = k.sb("wkv", [D, 3 * D])
    wout = k.sb("wout", [D, D])
    cosT, sinT = k.sb("cosT", [D, T]), k.sb("sinT", [D, T])
    cos, sin = k.sb("cos", [P, T]), k.sb("sin", [P, T])
    same_head = k.sb("same_head", [P, P])
    q1, q2 = k.sb("q1", [D, T]), k.sb("q2", [D, T])
    qlow, qexp = k.sb("qlow", [D, T]), k.sb("qexp", [D, T])
    k1, k2 = k.sb("k1", [P, T]), k.sb("k2", [P, T])
    klow, kexp = k.sb("klow", [P, T]), k.sb("kexp", [P, T])
    v1 = k.sb("v1", [P, J, D + 1])
    kvm, ksm = k.sb("kvm", [D, D]), k.sb("ksm", [D, D])
    den, rden, oT = k.sb("den", [D, T]), k.sb("rden", [D, T]), k.sb("oT", [D, T])
    chain = k.sem("chain")
    loaded, ones_ready = k.sem("loaded"), k.sem("ones_ready")
    q_in_psum, kv_in_psum = k.sem("q_in_psum"), k.sem("kv_in_psum")
    k_read, v_read = k.sem("k_read"), k.sem("v_read")
    qlow_ready, qexp_ready, q_ready = k.sem("qlow_ready"), k.sem("qexp_ready"), k.sem("q_ready")
    klow_ready, kexp_ready, k_ready = k.sem("klow_ready"), k.sem("kexp_ready"), k.sem("k_ready")
    kv_sum, kv_masked, ratio_in_psum = k.sem("kv_sum"), k.sem("kv_masked"), k.sem("ratio_in_psum")
    oT_ready, out_in_psum, x_updated = k.sem("oT_ready"), k.sem("out_in_psum"), k.sem("x_updated")
    loads = [(wq[:], dram["wq0"]), (wkv[:], dram["wkv0"]), (wout[:], dram["wout0"]), (cosT[:], dram["cosT"]),
             (sinT[:], dram["sinT"]), (cos[:], dram["cos"]), (sin[:], dram["sin"]), (same_head[:], dram["same_head"])]
    qp, rp = ps[:, 2 * BANK:4 * BANK], ps[:, 4 * BANK:6 * BANK]
    op = ps[:, 6 * BANK:8 * BANK]

    with nc.Block() as block:
        @block.sync
        def _(sp):
            for to, of in loads:
                sp.dma_start(to, of).then_inc(loaded, 16)

        @block.gpsimd
        def _(pool):
            nc.gpsimd.memset(v1[:, :, D:D + 1], 1.0).then_inc(ones_ready, 1)
            with pool.Fori(0, B) as b:
                norm.pool(pool, b)

        @block.vector
        def _(dve):
            link = Chain(dve, chain)
            v = nc.vector
            dve.wait_ge(loaded, 16 * len(loads))
            with dve.Fori(0, B) as b:
                link.restart()
                norm.vector(dve, link, b, x)
                dve.wait_ge(q_in_psum, b + 1)
                link(v.tensor_tensor(q1[:], qp, cosT[:], ALU.mult))
                link(v.tensor_tensor(q2[:], rp, sinT[:], ALU.mult))
                link(v.tensor_tensor(q1[:], q1[:], q2[:], ALU.add))
                v.tensor_scalar(qlow[:], q1[:], SCALE, 0.0, ALU.mult, ALU.min).then_inc(qlow_ready, 1)
                link(v.tensor_scalar(q1[:], q1[:], SCALE, 0.0, ALU.mult, ALU.max))
                for r in range(J):
                    dve.wait_ge(kv_in_psum, b * J + r + 1)
                    kp = ps[:, (6 + r % 2) * BANK:(6 + r % 2) * BANK + 3 * D]
                    link(v.tensor_tensor(k1[:, r * D:(r + 1) * D], kp[:, 0:D], cos[:, r * D:(r + 1) * D], ALU.mult))
                    v.tensor_tensor(k2[:, r * D:(r + 1) * D], kp[:, D:2 * D], sin[:, r * D:(r + 1) * D],
                                    ALU.mult).then_inc(k_read, 1)
                dve.wait_ge(k_read, b * J + J)
                link(v.tensor_tensor(k1[:], k1[:], k2[:], ALU.add))
                v.tensor_scalar(klow[:], k1[:], 0.0, None, ALU.min).then_inc(klow_ready, 1)
                link(v.tensor_scalar(k1[:], k1[:], 0.0, None, ALU.max))
                dve.wait_ge(qexp_ready, b + 1)
                v.tensor_tensor(q1[:], q1[:], qexp[:], ALU.add).then_inc(q_ready, 1)
                dve.wait_ge(kexp_ready, b + 1)
                v.tensor_tensor(k1[:], k1[:], kexp[:], ALU.add).then_inc(k_ready, 1)
                dve.wait_ge(kv_sum, b + 1)
                v.tensor_tensor(kvm[:], ps[:, 0:D], same_head[:], ALU.mult)
                v.tensor_scalar(ksm[:], same_head[:], ps[:, D:D + 1], None, ALU.mult).then_inc(kv_masked, 1)
                dve.wait_ge(ratio_in_psum, b + 1)
                link(v.tensor_scalar(den[:], rp, 1e-6, None, ALU.max))
                link(v.reciprocal(rden[:], den[:]))
                v.tensor_tensor(oT[:], qp, rden[:], ALU.mult).then_inc(oT_ready, 1)
                dve.wait_ge(out_in_psum, b + 1)
                v.tensor_tensor(rows_of(x, b), rows_of(x, b), op, ALU.add).then_inc(x_updated, 1)

        @block.scalar
        def _(act):
            with act.Fori(0, B) as b:
                norm.scalar(act, b, out_in_psum)
                act.wait_ge(qlow_ready, b + 1)
                nc.scalar.activation(qexp[:], qlow[:], ACT.Exp).then_inc(qexp_ready, 1)
                act.wait_ge(k_ready, b)
                act.wait_ge(kv_sum, b)
                for r in range(J):
                    act.wait_ge(k_read, b * J + r + 1)
                    at = (6 + r % 2) * BANK + 2 * D
                    nc.scalar.copy(v1[:, r, 0:D], ps[:, at:at + D]).then_inc(v_read, 1)
                act.wait_ge(klow_ready, b + 1)
                nc.scalar.activation(kexp[:], klow[:], ACT.Exp).then_inc(kexp_ready, 1)

        @block.tensor
        def _(pe):
            mm = nc.tensor.matmul
            pe.wait_ge(loaded, 16 * len(loads))
            pe.wait_ge(ones_ready, 1)
            with pe.Fori(0, B) as b:
                pe.wait_ge(kv_masked, b)
                norm.tensor(pe, b)
                pe.wait_ge(norm.xT_ready, b + 1)
                pe.wait_ge(oT_ready, b)
                for h in range(2):
                    c = slice(h * BANK, (h + 1) * BANK)
                    mm(qp[:, c], wq[:, 0:D], norm.xT[:, c], start=True, stop=True)
                    last = mm(rp[:, c], wq[:, D:2 * D], norm.xT[:, c], start=True, stop=True)
                last.then_inc(q_in_psum, 1)
                pe.wait_ge(x_updated, b)
                for r in range(J):
                    if r >= 2:
                        pe.wait_ge(k_read, b * J + r - 1)
                        pe.wait_ge(v_read, b * J + r - 1)
                    kp = ps[:, (6 + r % 2) * BANK:(6 + r % 2) * BANK + 3 * D]
                    last = mm(kp, norm.xT[:, r * P:(r + 1) * P], wkv[:], start=True, stop=True)
                    last.then_inc(kv_in_psum, 1)
                last = None
                pe.wait_ge(k_ready, b + 1)
                pe.wait_ge(v_read, b * J + J)
                for r in range(J):
                    last = mm(ps[:, 0:D + 1], k1[:, r * D:(r + 1) * D], v1[:, r, :], start=(r == 0), stop=(r == J - 1))
                last.then_inc(kv_sum, 1)
                pe.wait_ge(kv_masked, b + 1)
                pe.wait_ge(q_ready, b + 1)
                for h in range(2):
                    c = slice(h * BANK, (h + 1) * BANK)
                    mm(qp[:, c], kvm[:], q1[:, c], start=True, stop=True)
                    last = mm(rp[:, c], ksm[:], q1[:, c], start=True, stop=True)
                last.then_inc(ratio_in_psum, 1)
                pe.wait_ge(oT_ready, b + 1)
                for j in range(J):
                    last = mm(op[:, j * D:(j + 1) * D], by_token(oT[:])[:, j, :], wout[:], start=True, stop=True)
                last.then_inc(out_in_psum, 1)


class Fp4:

    def __init__(self, k, widest):
        self.k, self.nc = k, k.nc
        n = widest // FP4_BLOCK
        self.scale, self.inverse = k.sb("scale", [P, n]), k.sb("inverse", [P, n])
        self.scaled, self.size = k.sb("scaled", [P, widest]), k.sb("size", [P, widest])
        self.sign = k.sb("sign", [P, widest], BF16)
        self.low, self.high = k.sb("low", [P, widest], BF16), k.sb("high", [P, widest], BF16)

    def scale_down(self, link, src, width, scaled_ready):
        v, n = self.nc.vector, width // FP4_BLOCK
        blocks = lambda ap: ap.rearrange("p (n c) -> p n c", c=FP4_BLOCK)
        link(v.tensor_reduce(self.scale[:, 0:n], blocks(src), AX.X, ALU.max, apply_absolute_value=True))
        link(v.tensor_scalar(self.scale[:, 0:n], self.scale[:, 0:n], 1.0 / 6.0, 1e-12, ALU.mult, ALU.max))
        link(v.reciprocal(self.inverse[:, 0:n], self.scale[:, 0:n]))
        v.tensor_tensor(blocks(self.scaled[:, 0:width]), blocks(src), along(self.inverse[:, 0:n], FP4_BLOCK),
                        ALU.mult).then_inc(scaled_ready, 1)

    def split(self, width, split_ready):
        self.nc.scalar.activation(self.size[:, 0:width], self.scaled[:, 0:width], ACT.Abs)
        self.nc.scalar.activation(self.sign[:, 0:width], self.scaled[:, 0:width], ACT.Sign).then_inc(split_ready, 1)

    def round(self, link, dst, width):
        v, n = self.nc.vector, width // FP4_BLOCK
        size, low, high = self.size[:, 0:width], self.low[:, 0:width], self.high[:, 0:width]
        link(v.tensor_scalar(high, size, 5.0, 2.0, ALU.is_gt, ALU.mult))
        link(v.scalar_tensor_tensor(high, size, 3.5, high, ALU.is_gt, ALU.add))
        link(v.tensor_scalar(low, size, 0.25, None, ALU.is_gt))
        link(v.scalar_tensor_tensor(high, size, 2.5, high, ALU.is_gt, ALU.add))
        link(v.scalar_tensor_tensor(low, high, 2.0, low, ALU.mult, ALU.add))
        for middle_point in (0.75, 1.25, 1.75):
            link(v.scalar_tensor_tensor(low, size, middle_point, low, ALU.is_gt, ALU.add))
        link(v.scalar_tensor_tensor(low, low, 0.5, self.sign[:, 0:width], ALU.mult, ALU.mult))
        blocks = lambda ap: ap.rearrange("p (n c) -> p n c", c=FP4_BLOCK)
        return v.tensor_tensor(blocks(dst), blocks(low), along(self.scale[:, 0:n], FP4_BLOCK), ALU.mult)


CHUNKS = [(0, 128), (128, 128), (256, 96)]


def fp4_weights(nc, k, x):
    ps = k.ps
    raw = k.sb("raw", [P, 6 * D + FF4])
    quantized = k.sb("quantized", [P, 6 * D + FF4])
    fp4 = Fp4(k, 6 * D + FF4)
    cleared, loaded, chain = k.sem("cleared"), k.sem("loaded"), k.sem("chain")
    scaled_ready, split_ready, quantized_ready = k.sem("scaled_ready"), k.sem("split_ready"), k.sem("quantized_ready")
    in_psum, copied = k.sem("in_psum"), k.sem("copied")
    width = 6 * D + FF4

    with nc.Block() as block:
        @block.gpsimd
        def _(pool):
            nc.gpsimd.memset(raw[:], 0.0).then_inc(cleared, 1)

        @block.sync
        def _(sp):
            sp.wait_ge(cleared, 1)
            for m, name in enumerate(("wgate", "wup")):
                for c, (r, n) in enumerate(CHUNKS):
                    at = (3 * m + c) * D
                    sp.dma_start(raw[0:n, at:at + D], k.dram[name][r:r + n, :]).then_inc(loaded, 16)
            sp.dma_start(raw[:, 6 * D:width], k.dram["wdown"]).then_inc(loaded, 16)

        @block.vector
        def _(dve):
            link = Chain(dve, chain)
            dve.wait_ge(loaded, 16 * 7)
            fp4.scale_down(link, raw[:], width, scaled_ready)
            dve.wait_ge(split_ready, 1)
            fp4.round(link, quantized[:], width).then_inc(quantized_ready, 1)

        @block.scalar
        def _(act):
            act.wait_ge(scaled_ready, 1)
            fp4.split(width, split_ready)
            for m, to in enumerate((k.wgateT, k.wupT, k.wdownT)):
                act.wait_ge(in_psum, m + 1)
                last = nc.scalar.copy(to[:], ps[:, m * BANK:m * BANK + (FF4 if m < 2 else 3 * P)])
            last.then_inc(copied, 1)
            act.wait_ge(copied, 1)

        @block.tensor
        def _(pe):
            pe.wait_ge(quantized_ready, 1)
            for m in range(2):
                for c, (r, n) in enumerate(CHUNKS):
                    at = (3 * m + c) * D
                    last = nc.tensor.transpose(ps[:, m * BANK + r:m * BANK + r + n], quantized[0:n, at:at + D],
                                               k.ident[0:n, 0:n])
                last.then_inc(in_psum, 1)
            nc.tensor.matmul(ps[:, 2 * BANK + 2 * P:2 * BANK + 3 * P], k.zeros[:], k.ident[:], start=True, stop=True)
            for c, (r, n) in enumerate(CHUNKS):
                last = nc.tensor.transpose(ps[0:n, 2 * BANK + c * P:2 * BANK + (c + 1) * P],
                                           quantized[:, 6 * D + r:6 * D + r + n], k.ident[:])
            last.then_inc(in_psum, 1)


def fp4_ffn(nc, k, x):
    ps = k.ps
    norm = Norm(k, ps[:, 0:2 * BANK])
    fp4 = Fp4(k, J * FF4)
    xq, hidden, hq = k.sb("xq", [P, J * D]), k.sb("hidden", [P, J * FF4]), k.sb("hq", [P, J * FF4])
    gate = k.sb("gate", [P, 2, FF4])
    hqT = k.sb("hqT", [P, 2, 3 * P])
    chain = k.sem("chain")
    xscaled, xsplit, xq_ready = k.sem("xscaled"), k.sem("xsplit"), k.sem("xq_ready")
    hscaled, hsplit, hq_ready = k.sem("hscaled"), k.sem("hsplit"), k.sem("hq_ready")
    gate_in_psum, gate_ready, hidden_ready = k.sem("gate_in_psum"), k.sem("gate_ready"), k.sem("hidden_ready")
    hT_in_psum, hT_ready, out_in_psum, x_updated = (k.sem("hT_in_psum"), k.sem("hT_ready"),
                                                    k.sem("out_in_psum"), k.sem("x_updated"))
    op = ps[:, 0:2 * BANK]
    norm.xn_ready, xn_ready = xq_ready, norm.xn_ready
    norm.xn, xn = xq, norm.xn

    with nc.Block() as block:
        @block.gpsimd
        def _(pool):
            with pool.Fori(0, B) as b:
                norm.pool(pool, b)

        @block.vector
        def _(dve):
            link = Chain(dve, chain)
            v = nc.vector
            with dve.Fori(0, B) as b:
                link.restart()
                norm.xn, norm.xn_ready = xn, xn_ready
                norm.vector(dve, link, b, x)
                norm.xn, norm.xn_ready = xq, xq_ready
                dve.wait_ge(xn_ready, b + 1)
                fp4.scale_down(link, xn[:], J * D, xscaled)
                dve.wait_ge(xsplit, b + 1)
                fp4.round(link, xq[:], J * D).then_inc(xq_ready, 1)
                for j in range(J):
                    up = ps[:, (3 + 2 * (j % 2)) * BANK:(3 + 2 * (j % 2)) * BANK + FF4]
                    dve.wait_ge(gate_ready, b * J + j + 1)
                    v.tensor_tensor(hidden[:, j * FF4:(j + 1) * FF4], gate[:, j % 2, :], up, ALU.mult).then_inc(hidden_ready, 1)
                dve.wait_ge(hidden_ready, b * J + J)
                fp4.scale_down(link, hidden[:], J * FF4, hscaled)
                dve.wait_ge(hsplit, b + 1)
                fp4.round(link, hq[:], J * FF4).then_inc(hq_ready, 1)
                dve.wait_ge(out_in_psum, b + 1)
                v.tensor_tensor(rows_of(x, b), rows_of(x, b), op, ALU.add).then_inc(x_updated, 1)

        @block.scalar
        def _(act):
            with act.Fori(0, B) as b:
                act.wait_ge(xscaled, b + 1)
                fp4.split(J * D, xsplit)
                act.wait_ge(norm.xT_in_psum, b + 1)
                act.wait_ge(out_in_psum, b)
                for h in range(2):
                    last = nc.scalar.copy(norm.xT[:, h * BANK:(h + 1) * BANK], ps[:, h * BANK:(h + 1) * BANK])
                last.then_inc(norm.xT_ready, 1)
                for j in range(J):
                    act.wait_ge(gate_in_psum, b * J + j + 1)
                    if j >= 2:
                        act.wait_ge(hidden_ready, b * J + j - 1)
                    nc.scalar.activation(gate[:, j % 2, :], ps[:, (2 + 2 * (j % 2)) * BANK:(2 + 2 * (j % 2)) * BANK + FF4],
                                         ACT.Silu).then_inc(gate_ready, 1)
                act.wait_ge(hscaled, b + 1)
                fp4.split(J * FF4, hsplit)
                for j in range(J):
                    act.wait_ge(hT_in_psum, b * J + j + 1)
                    at = (6 + j % 2) * BANK
                    nc.scalar.copy(hqT[:, j % 2, 0:2 * P], ps[:, at:at + 2 * P])
                    nc.scalar.copy(hqT[0:96, j % 2, 2 * P:3 * P], ps[0:96, at + 2 * P:at + 3 * P]).then_inc(hT_ready, 1)

        @block.tensor
        def _(pe):
            with pe.Fori(0, B) as b:
                pe.wait_ge(x_updated, b)
                norm.tensor(pe, b)
                pe.wait_ge(norm.xT_ready, b + 1)
                for j in range(J):
                    if j >= 2:
                        pe.wait_ge(hidden_ready, b * J + j - 1)
                    at = (2 + 2 * (j % 2)) * BANK
                    xT = norm.xT[:, j * P:(j + 1) * P]
                    nc.tensor.matmul(ps[:, at:at + FF4], xT, k.wgateT[:], start=True, stop=True)
                    last = nc.tensor.matmul(ps[:, at + BANK:at + BANK + FF4], xT, k.wupT[:], start=True, stop=True)
                    last.then_inc(gate_in_psum, 1)
                pe.wait_ge(hq_ready, b + 1)

                def transpose_hidden(j):
                    if j >= 2:
                        pe.wait_ge(hT_ready, b * J + j - 1)
                    for c, (r, n) in enumerate(CHUNKS):
                        at = (6 + j % 2) * BANK + c * P
                        last = nc.tensor.transpose(ps[0:n, at:at + P], hq[:, j * FF4 + r:j * FF4 + r + n], k.ident[:])
                    last.then_inc(hT_in_psum, 1)

                transpose_hidden(0)
                for j in range(J):
                    if j + 1 < J:
                        transpose_hidden(j + 1)
                    pe.wait_ge(hT_ready, b * J + j + 1)
                    for c, (r, n) in enumerate(CHUNKS):
                        last = nc.tensor.matmul(op[:, j * D:(j + 1) * D], hqT[0:n, j % 2, c * P:(c + 1) * P],
                                                k.wdownT[0:n, c * D:(c + 1) * D], start=(c == 0), stop=(c == 2))
                last.then_inc(out_in_psum, 1)


def low_rank_ffn(nc, k, x):
    ps = k.ps
    norm = Norm(k, ps[:, 0:2 * BANK])
    nf = FFL // P
    u1, v1, b1 = k.sb("u1", [D, RANK]), k.sb("v1", [RANK, FFL]), k.sb("b1", [P, nf])
    u2 = k.sb("u2", [P, nf, RANK])
    v2 = k.sb("v2", [RANK + 1, D])
    pT, hT = k.sb("pT", [RANK, T]), k.sb("hT", [P, 2, BANK])
    qT = k.sb("qT", [RANK + 1, T])
    chain, loaded, ones_ready = k.sem("chain"), k.sem("loaded"), k.sem("ones_ready")
    p_in_psum, p_ready = k.sem("p_in_psum"), k.sem("p_ready")
    h_in_psum, h_ready, h_used = k.sem("h_in_psum"), k.sem("h_ready"), k.sem("h_used")
    q_ready, out_in_psum, x_updated = k.sem("q_ready"), k.sem("out_in_psum"), k.sem("x_updated")
    d = k.dram
    loads = [(u1[:], d["u1"]), (v1[:], d["v1"]), (b1[:], d["b1"].rearrange("(c p) -> p c", p=P)),
             (u2[:], d["u2"].rearrange("(c p) r -> p c r", p=P)), (v2[:], d["v2"])]
    pp, qp, op = ps[0:RANK, 2 * BANK:4 * BANK], ps[0:RANK, 6 * BANK:8 * BANK], ps[:, 0:2 * BANK]

    with nc.Block() as block:
        @block.sync
        def _(sp):
            with nc.allow_non_contiguous_dma("biases, once"):
                for to, of in loads:
                    sp.dma_start(to, of).then_inc(loaded, 16)

        @block.gpsimd
        def _(pool):
            nc.gpsimd.memset(qT[RANK:RANK + 1, :], 1.0).then_inc(ones_ready, 1)
            pool.wait_ge(ones_ready, 1)
            with pool.Fori(0, B) as b:
                norm.pool(pool, b)

        @block.vector
        def _(dve):
            link = Chain(dve, chain)
            with dve.Fori(0, B) as b:
                link.restart()
                norm.vector(dve, link, b, x, norm.xT_in_psum)
                dve.wait_ge(p_in_psum, b + 1)
                nc.vector.tensor_copy(pT[:], pp).then_inc(p_ready, 1)
                dve.wait_ge(h_used, b * 2 * nf + 2 * nf)
                nc.vector.tensor_copy(qT[0:RANK, :], qp).then_inc(q_ready, 1)
                dve.wait_ge(out_in_psum, b + 1)
                nc.vector.tensor_tensor(rows_of(x, b), rows_of(x, b), op, ALU.add).then_inc(x_updated, 1)

        @block.scalar
        def _(act):
            act.wait_ge(loaded, 16 * len(loads))
            with act.Fori(0, B) as b:
                norm.scalar(act, b, p_in_psum)
                for u in range(2 * nf):
                    act.wait_ge(h_in_psum, b * 2 * nf + u + 1)
                    if u >= 2:
                        act.wait_ge(h_used, b * 2 * nf + u - 1)
                    nc.scalar.activation(hT[:, u % 2, :], ps[:, (4 + u % 2) * BANK:(5 + u % 2) * BANK], ACT.Gelu_apprx_tanh,
                                         bias=b1[:, u % nf:u % nf + 1]).then_inc(h_ready, 1)

        @block.tensor
        def _(pe):
            mm = nc.tensor.matmul
            pe.wait_ge(loaded, 16 * len(loads))
            pe.wait_ge(ones_ready, 1)
            with pe.Fori(0, B) as b:
                pe.wait_ge(x_updated, b)
                norm.tensor(pe, b)
                pe.wait_ge(norm.xT_ready, b + 1)
                for h in range(2):
                    last = mm(pp[:, h * BANK:(h + 1) * BANK], u1[:], norm.xT[:, h * BANK:(h + 1) * BANK], start=True, stop=True)
                last.then_inc(p_in_psum, 1)
                pe.wait_ge(p_ready, b + 1)

                def up(u):
                    if u >= 2:
                        pe.wait_ge(h_ready, b * 2 * nf + u - 1)
                    h, c = u // nf, u % nf
                    mm(ps[:, (4 + u % 2) * BANK:(5 + u % 2) * BANK], v1[:, c * P:(c + 1) * P],
                       pT[:, h * BANK:(h + 1) * BANK], start=True, stop=True).then_inc(h_in_psum, 1)

                up(0)
                for u in range(2 * nf):
                    if u + 1 < 2 * nf:
                        up(u + 1)
                    h, c = u // nf, u % nf
                    pe.wait_ge(h_ready, b * 2 * nf + u + 1)
                    last = mm(qp[:, h * BANK:(h + 1) * BANK], u2[:, c, :], hT[:, u % 2, :], start=(c == 0), stop=(c == nf - 1))
                    last.then_inc(h_used, 1)
                pe.wait_ge(q_ready, b + 1)
                for j in range(J):
                    last = mm(op[:, j * D:(j + 1) * D], by_token(qT[:])[:, j, :], v2[:], start=True, stop=True)
                last.then_inc(out_in_psum, 1)



def mamba(nc, k, x):
    ps = k.ps
    norm = Norm(k, ps[:, 0:2 * BANK])
    nch = E_IN // P
    win = k.sb("win", [D, 2 * E_IN])
    wx = k.sb("wx", [P, nch, E_IN + 3 * 2 * NS])
    wout = k.sb("wout", [P, nch, D])
    cw, cb = k.sb("cw", [P, nch, KCONV]), k.sb("cb", [P, nch])
    skip, a_neg = k.sb("skip", [P, nch]), k.sb("a_neg", [P, nch, NS])
    pick = k.sb("pick", [3 * 2 * NS, 2 * NS, P], BF16)
    pad = KCONV - 1
    xin = k.sb("xin", [P, nch, pad + T])
    z, hc = k.sb("z", [P, nch, T]), k.sb("hc", [P, nch, T])
    conv = k.sb("conv", [P, nch, T])
    mag, soft = k.sb("mag", [P, nch, T]), k.sb("soft", [P, nch, T])
    delta, du = k.sb("delta", [P, nch, T]), k.sb("du", [P, nch, T])
    bc, bc3 = k.sb("bc", [3 * 2 * NS, T]), k.sb("bc3", [3 * 2 * NS, T], BF16)
    decay, gain = k.sb("decay", [P, nch, T]), k.sb("gain", [P, nch, T])
    state, seen = k.sb("state", [P, nch, T]), k.sb("seen", [P, nch, T])
    y = k.sb("y", [P, nch, T])
    S = k.sem
    chain, loaded, pad_ready, a_ready = S("chain"), S("loaded"), S("pad_ready"), S("a_ready")
    achain = S("achain")
    xz_in_psum, xin_ready, z_ready, conv_ready = S("xz_in_psum"), S("xin_ready"), S("z_ready"), S("conv_ready")
    hc_ready, dt_in_psum, bc_in_psum, bc_copied, bc3_ready = (S("hc_ready"), S("dt_in_psum"), S("bc_in_psum"),
                                                              S("bc_copied"), S("bc3_ready"))
    mag_ready, soft_ready, delta_ready = S("mag_ready"), S("soft_ready"), S("delta_ready")
    decay_ready, b_in_psum, c_in_psum = S("decay_ready"), S("b_in_psum"), S("c_in_psum")
    gain_ready, state_ready, seen_ready, seen_used = S("gain_ready"), S("state_ready"), S("seen_ready"), S("seen_used")
    y_in_psum, y_ready, out_in_psum, x_updated = S("y_in_psum"), S("y_ready"), S("out_in_psum"), S("x_updated")
    d = k.dram
    loads = [(win[:], d["win"]), (wx[:], d["wx"].rearrange("(c p) n -> p c n", p=P)),
             (wout[:], d["wout3"].rearrange("(c p) n -> p c n", p=P)),
             (cw[:], d["cw"].rearrange("(c p) n -> p c n", p=P)), (cb[:], d["cb"].rearrange("(c p) -> p c", p=P)),
             (skip[:], d["skip"].rearrange("(c p) -> p c", p=P)),
             (a_neg[:], d["alog"].rearrange("(c p) n -> p c n", p=P)), (pick[:], d["pick"])]
    flat = lambda t: t[:].rearrange("p c t -> p (c t)")
    bp, cp, yp = ps[:, 0:2 * BANK], ps[:, 2 * BANK:4 * BANK], ps[:, 4 * BANK:8 * BANK]
    quarter = 4

    with nc.Block() as block:
        @block.sync
        def _(sp):
            with nc.allow_non_contiguous_dma("per-channel parameters, once"):
                for to, of in loads:
                    sp.dma_start(to, of).then_inc(loaded, 16)

        @block.gpsimd
        def _(pool):
            nc.gpsimd.memset(xin[:, :, 0:pad], 0.0).then_inc(pad_ready, 1)
            with pool.Fori(0, B) as b:
                norm.pool(pool, b)

        @block.vector
        def _(dve):
            link = Chain(dve, chain)
            v = nc.vector
            dve.wait_ge(loaded, 16 * len(loads))
            dve.wait_ge(a_ready, 1)
            dve.wait_ge(pad_ready, 1)
            link(v.tensor_scalar(a_neg[:], a_neg[:], -1.0, None, ALU.mult))
            v.tensor_copy(mag[:, 0, 0:1], a_neg[:, 0, 0:1]).then_inc(a_ready, 1)
            with dve.Fori(0, B) as b:
                link.restart()
                norm.vector(dve, link, b, x)
                dve.wait_ge(xin_ready, b * nch + nch)
                for c in range(nch):
                    link(v.tensor_scalar(conv[:, c, :], xin[:, c, 0:T], cw[:, c, 0:1], None, ALU.mult))
                    for tap in range(1, KCONV):
                        ins = v.scalar_tensor_tensor(conv[:, c, :], xin[:, c, tap:tap + T], cw[:, c, tap:tap + 1],
                                                     conv[:, c, :], ALU.mult, ALU.add)
                        if tap < KCONV - 1:
                            link(ins)
                    ins.then_inc(conv_ready, 1)
                dve.wait_ge(bc_copied, b + 1)
                dve.wait_ge(seen_used, b * 2 * NS)
                n2 = 2 * NS
                link(v.tensor_copy(bc3[:], bc[:]))
                link(v.tensor_tensor(bc[n2:2 * n2], bc[n2:2 * n2], bc3[n2:2 * n2], ALU.subtract))
                link(v.tensor_tensor(bc[2 * n2:3 * n2], bc[2 * n2:3 * n2], bc3[2 * n2:3 * n2], ALU.subtract))
                link(v.tensor_copy(bc3[n2:2 * n2], bc[n2:2 * n2]))
                link(v.tensor_copy(bc3[2 * n2:3 * n2], bc[2 * n2:3 * n2]))
                link(v.tensor_tensor(bc[2 * n2:3 * n2], bc[2 * n2:3 * n2], bc3[2 * n2:3 * n2], ALU.subtract))
                v.tensor_copy(bc3[2 * n2:3 * n2], bc[2 * n2:3 * n2]).then_inc(bc3_ready, 1)
                dve.wait_ge(dt_in_psum, b + 1)
                dve.wait_ge(mag_ready, b + 1)
                link(v.tensor_scalar(flat(delta), yp, 0.0, None, ALU.max))
                dve.wait_ge(soft_ready, b + 1)
                v.tensor_tensor(flat(delta), flat(delta), flat(soft), ALU.add).then_inc(delta_ready, 1)
                dve.wait_ge(delta_ready, b + 1)
                link(v.tensor_tensor(flat(du), flat(delta), flat(hc), ALU.mult))
                with dve.Fori(0, NS) as n:
                    i = b * NS + n
                    dve.wait_ge(b_in_psum, i + 1)
                    for c in range(nch):
                        v.tensor_tensor(gain[:, c, :], du[:, c, :], bp, ALU.mult).then_inc(gain_ready, 1)
                    dve.wait_ge(c_in_psum, i + 1)
                    for c in range(nch):
                        dve.wait_ge(gain_ready, 2 * i + 1 + c)
                        dve.wait_ge(decay_ready, 2 * i + 1 + c)
                        v.tensor_tensor_scan(state[:, c, :], decay[:, c, :], gain[:, c, :], 0.0, ALU.mult,
                                             ALU.add).then_inc(state_ready, 1)
                        dve.wait_ge(state_ready, 2 * i + 1 + c)
                        dve.wait_ge(seen_used, 2 * i)
                        v.tensor_tensor(seen[:, c, :], state[:, c, :], cp, ALU.mult).then_inc(seen_ready, 1)
                dve.wait_ge(y_in_psum, b + 1)
                for c in range(nch):
                    v.scalar_tensor_tensor(y[:, c, :], hc[:, c, :], skip[:, c:c + 1], yp[:, c * T:(c + 1) * T],
                                           ALU.mult, ALU.add).then_inc(chain, 1)
                link.n += nch
                dve.wait_ge(chain, link.n)
                v.tensor_tensor(flat(y), flat(y), flat(z), ALU.mult).then_inc(y_ready, 1)
                dve.wait_ge(out_in_psum, b + 1)
                v.tensor_tensor(rows_of(x, b), rows_of(x, b), bp, ALU.add).then_inc(x_updated, 1)

        @block.scalar
        def _(act):
            link = Chain(act, achain)
            act.wait_ge(loaded, 16 * len(loads))
            nc.scalar.activation(a_neg[:], a_neg[:], ACT.Exp).then_inc(a_ready, 1)
            act.wait_ge(a_ready, 2)
            act.wait_ge(pad_ready, 1)
            with act.Fori(0, B) as b:
                link.restart()
                norm.scalar(act, b, out_in_psum)
                for m in range(quarter):
                    act.wait_ge(xz_in_psum, b * quarter + m + 1)
                    of = ps[:, (4 + 2 * (m % 2)) * BANK:(6 + 2 * (m % 2)) * BANK]
                    if m < nch:
                        nc.scalar.copy(xin[:, m, pad:pad + T], of).then_inc(xin_ready, 1)
                    else:
                        nc.scalar.activation(z[:, m - nch, :], of, ACT.Silu).then_inc(z_ready, 1)
                for c in range(nch):
                    act.wait_ge(conv_ready, b * nch + c + 1)
                    nc.scalar.activation(hc[:, c, :], conv[:, c, :], ACT.Silu, bias=cb[:, c:c + 1]).then_inc(hc_ready, 1)
                act.wait_ge(bc_in_psum, b + 1)
                nc.scalar.copy(bc[:], ps[0:3 * 2 * NS, 2 * BANK:4 * BANK]).then_inc(bc_copied, 1)
                act.wait_ge(dt_in_psum, b + 1)
                nc.scalar.activation(flat(mag), yp, ACT.Abs).then_inc(mag_ready, 1)
                act.wait_ge(mag_ready, b + 1)
                link(nc.scalar.activation(flat(mag), flat(mag), ACT.Exp, scale=-1.0))
                nc.scalar.activation(flat(soft), flat(mag), ACT.Ln, bias=1.0).then_inc(soft_ready, 1)
                act.wait_ge(delta_ready, b + 1)
                with act.Fori(0, NS) as n:
                    i = b * NS + n
                    for c in range(nch):
                        act.wait_ge(state_ready, 2 * i)
                        nc.scalar.activation(decay[:, c, :], delta[:, c, :], ACT.Exp,
                                             scale=a_neg[:, c, bass.ds(n, 1)]).then_inc(decay_ready, 1)

        @block.tensor
        def _(pe):
            mm = nc.tensor.matmul
            pe.wait_ge(loaded, 16 * len(loads))
            with pe.Fori(0, B) as b:
                pe.wait_ge(x_updated, b)
                norm.tensor(pe, b)
                pe.wait_ge(norm.xT_ready, b + 1)
                for m in range(quarter):
                    at = (4 + 2 * (m % 2)) * BANK
                    if m == 2:
                        pe.wait_ge(xin_ready, b * nch + 1)
                    elif m == 3:
                        pe.wait_ge(xin_ready, b * nch + 2)
                    for h in range(2):
                        last = mm(ps[:, at + h * BANK:at + (h + 1) * BANK], win[:, m * P:(m + 1) * P],
                                  norm.xT[:, h * BANK:(h + 1) * BANK], start=True, stop=True)
                    last.then_inc(xz_in_psum, 1)
                pe.wait_ge(hc_ready, b * nch + nch)
                pe.wait_ge(z_ready, b * nch + nch)
                n3 = 3 * 2 * NS
                for h in range(2):
                    for c in range(nch):
                        last = mm(ps[0:n3, (2 + h) * BANK:(3 + h) * BANK], wx[:, c, E_IN:E_IN + n3],
                                  hc[:, c, h * BANK:(h + 1) * BANK], start=(c == 0), stop=(c == nch - 1))
                last.then_inc(bc_in_psum, 1)
                for o in range(nch):
                    for h in range(2):
                        for c in range(nch):
                            at = (4 + 2 * o + h) * BANK
                            last = mm(ps[:, at:at + BANK], wx[:, c, o * P:(o + 1) * P],
                                      hc[:, c, h * BANK:(h + 1) * BANK], start=(c == 0), stop=(c == nch - 1))
                last.then_inc(dt_in_psum, 1)
                pe.wait_ge(bc3_ready, b + 1)
                pe.wait_ge(delta_ready, b + 1)
                for q in range(4):
                    mm(yp[:, q * BANK:(q + 1) * BANK], k.zeros[:], norm.xT[:, 0:BANK], start=True, stop=True)
                with pe.Fori(0, NS) as n:
                    i = b * NS + n
                    pe.wait_ge(gain_ready, 2 * i)
                    for h in range(2):
                        last = mm(bp[:, h * BANK:(h + 1) * BANK], pick[:, bass.ds(n, 1), :].rearrange("k o p -> k (o p)"),
                                  bc3[:, h * BANK:(h + 1) * BANK], start=True, stop=True)
                    last.then_inc(b_in_psum, 1)
                    pe.wait_ge(seen_ready, 2 * i)
                    for h in range(2):
                        last = mm(cp[:, h * BANK:(h + 1) * BANK], pick[:, bass.ds(n + NS, 1), :].rearrange("k o p -> k (o p)"),
                                  bc3[:, h * BANK:(h + 1) * BANK], start=True, stop=True)
                    last.then_inc(c_in_psum, 1)
                    for c in range(nch):
                        pe.wait_ge(seen_ready, 2 * i + c + 1)
                        for h in range(2):
                            last = mm(yp[:, (2 * c + h) * BANK:(2 * c + h + 1) * BANK], k.ident[:],
                                      seen[:, c, h * BANK:(h + 1) * BANK], start=False, stop=True, skip_group_check=True)
                        last.then_inc(seen_used, 1)
                for q in range(4):
                    last = mm(yp[:, q * BANK:(q + 1) * BANK], k.zeros[:], norm.xT[:, 0:BANK], start=False, stop=True,
                              skip_group_check=True)
                last.then_inc(y_in_psum, 1)
                pe.wait_ge(y_ready, b + 1)
                for j in range(J):
                    for c in range(nch):
                        last = mm(bp[:, j * D:(j + 1) * D], by_token(y[:, c, :])[:, j, :], wout[:, c, :],
                                  start=(c == 0), stop=(c == nch - 1))
                last.then_inc(out_in_psum, 1)



def split_rows(nc, k, link, src, parts, n):
    for part in range(3):
        ins = nc.vector.tensor_copy(parts[0:n, part, :], src)
        if part == 2:
            return ins
        link(ins)
        link(nc.vector.tensor_tensor(src, src, parts[0:n, part, :], ALU.subtract))


def project_topk(nc, k, x, q_parts, k_parts, v1):
    ps = k.ps
    norm = Norm(k, ps[:, 0:2 * BANK])
    kvw = NKV * HD
    width, nrm = D + 2 * kvw, D + kvw
    heads = nrm // HD
    wqkv, bias = k.sb("wqkv", [D, width]), k.sb("bias", [P, width])
    gain = k.sb("gain", [P, nrm])
    qkv, sq = k.sb("qkv", [P, J, width]), k.sb("sq", [P, J, nrm])
    ms, mse, rs = k.sb("ms", [P, J * heads]), k.sb("mse", [P, J * heads]), k.sb("rs", [P, J * heads])
    qT, kT = k.sb("qT", [D, T]), k.sb("kT", [kvw, T])
    qs, ks = k.sb("qs", [D, 3, T], BF16), k.sb("ks", [kvw, 3, T], BF16)
    S = k.sem
    chain, loaded, ones_ready = S("chain"), S("loaded"), S("ones_ready")
    qkv_in_psum, qkv_read, ms_ready, rs_ready = S("qkv_in_psum"), S("qkv_read"), S("ms_ready"), S("rs_ready")
    qk_ready, qkT_in_psum, qT_ready, kT_ready = S("qk_ready"), S("qkT_in_psum"), S("qT_ready"), S("kT_ready")
    qs_ready, ks_ready, v_ready, stored = S("qs_ready"), S("ks_ready"), S("v_ready"), S("stored")
    d = k.dram
    loads = [(wqkv[:], d["wqkv5"]), (bias[:], d["bqkv5"].partition_broadcast(P)), (gain[:], d["gain5"].partition_broadcast(P))]

    with nc.Block() as block:
        @block.sync
        def _(sp):
            for to, of in loads:
                sp.dma_start(to, of).then_inc(loaded, 16)
            with sp.Fori(0, B) as b:
                sp.wait_ge(qs_ready, b + 1)
                sp.dma_start(q_parts[:, :, bass.ds(b * T, T)], qs[:]).then_inc(stored, 16)
                sp.wait_ge(ks_ready, b + 1)
                sp.dma_start(k_parts[0:kvw, :, bass.ds(b * T, T)], ks[:]).then_inc(stored, 16)
            sp.wait_ge(stored, 32 * B)

        @block.gpsimd
        def _(pool):
            nc.gpsimd.memset(v1[:, 0:B * J * NKV * (HD + 1)], 1.0).then_inc(ones_ready, 1)
            with pool.Fori(0, B) as b:
                norm.pool(pool, b)
                pool.wait_ge(ms_ready, b + 1)
                nc.gpsimd.tensor_tensor(rs[:], mse[:], k.minus_half[:], ALU.pow).then_inc(rs_ready, 1)

        @block.vector
        def _(dve):
            link = Chain(dve, chain)
            v = nc.vector
            dve.wait_ge(loaded, 16 * len(loads))
            dve.wait_ge(ones_ready, 1)
            link(v.tensor_scalar(gain[:, 0:D], gain[:, 0:D], SCALE, None, ALU.mult))
            with dve.Fori(0, B) as b:
                link.restart()
                norm.vector(dve, link, b, x)
                for r in range(J):
                    dve.wait_ge(qkv_in_psum, b * J + r + 1)
                    at = (2 + r % 2) * BANK
                    v.tensor_tensor(qkv[:, r, :], ps[:, at:at + width], bias[:], ALU.add).then_inc(qkv_read, 1)
                dve.wait_ge(qkv_read, b * J + J)
                row = J * NKV * (HD + 1)
                v.tensor_copy(v1[:, bass.ds(b * row, row)].rearrange("p (r g c) -> p r g c", r=J, g=NKV)[:, :, :, 0:HD],
                              qkv[:, :, nrm:width].rearrange("p r (g c) -> p r g c", c=HD)).then_inc(v_ready, 1)
                link(v.tensor_tensor(sq[:], qkv[:, :, 0:nrm], qkv[:, :, 0:nrm], ALU.mult))
                link(v.tensor_reduce(ms[:].rearrange("p (r h) -> p r h", r=J), sq[:].rearrange("p r (h c) -> p r h c", c=HD), AX.X, ALU.add))
                v.tensor_scalar(mse[:], ms[:], 1.0 / HD, RMS_EPS, ALU.mult, ALU.add).then_inc(ms_ready, 1)
                dve.wait_ge(rs_ready, b + 1)
                link(v.tensor_tensor(sq[:].rearrange("p r (h c) -> p (r h) c", c=HD) if False else sq[:].rearrange("p r (h c) -> p r h c", c=HD),
                                     qkv[:, :, 0:nrm].rearrange("p r (h c) -> p r h c", c=HD),
                                     rs[:].rearrange("p (r h) -> p r h", r=J).unsqueeze(3).broadcast_to([P, J, heads, HD]), ALU.mult))
                v.tensor_tensor(sq[:], sq[:], middle(gain[:], J), ALU.mult).then_inc(qk_ready, 1)
                dve.wait_ge(qT_ready, b + 1)
                dve.wait_ge(stored, 32 * b)
                split_rows(nc, k, link, qT[:], qs, D).then_inc(qs_ready, 1)
                dve.wait_ge(kT_ready, b + 1)
                split_rows(nc, k, link, kT[:], ks, kvw).then_inc(ks_ready, 1)

        @block.scalar
        def _(act):
            with act.Fori(0, B) as b:
                norm.scalar(act, b, qk_ready)
                act.wait_ge(qkT_in_psum, b + 1)
                act.wait_ge(ks_ready, b)
                nc.scalar.copy(qT[:], ps[:, 4 * BANK:6 * BANK]).then_inc(qT_ready, 1)
                nc.scalar.copy(kT[:], ps[0:kvw, 6 * BANK:8 * BANK]).then_inc(kT_ready, 1)

        @block.tensor
        def _(pe):
            pe.wait_ge(loaded, 16 * len(loads))
            with pe.Fori(0, B) as b:
                norm.tensor(pe, b)
                pe.wait_ge(norm.xT_ready, b + 1)
                for r in range(J):
                    if r >= 2:
                        pe.wait_ge(qkv_read, b * J + r - 1)
                    at = (2 + r % 2) * BANK
                    nc.tensor.matmul(ps[:, at:at + width], norm.xT[:, r * P:(r + 1) * P], wqkv[:], start=True,
                                     stop=True).then_inc(qkv_in_psum, 1)
                pe.wait_ge(qk_ready, b + 1)
                for r in range(J):
                    nc.tensor.transpose(ps[:, 4 * BANK + r * P:4 * BANK + (r + 1) * P], sq[:, r, 0:D], k.ident[:])
                    last = nc.tensor.transpose(ps[0:kvw, 6 * BANK + r * P:6 * BANK + (r + 1) * P], sq[:, r, D:nrm], k.ident[:])
                last.then_inc(qkT_in_psum, 1)


def project_causal(nc, k, x, q_parts, k_parts, v1):
    ps = k.ps
    norm = Norm(k, ps[:, 0:2 * BANK])
    wqkv = k.sb("wqkv", [D, 3 * D])
    qT, kT = k.sb("qT", [D, T]), k.sb("kT", [D, T])
    qs, ks = k.sb("qs", [D, 3, T], BF16), k.sb("ks", [D, 3, T], BF16)
    S = k.sem
    chain, loaded, ones_ready = S("chain"), S("loaded"), S("ones_ready")
    q_in_psum, v_in_psum, v_ready, qT_ready, kT_ready = (S("q_in_psum"), S("v_in_psum"), S("v_ready"), S("qT_ready"),
                                                         S("kT_ready"))
    qs_ready, ks_ready, stored = S("qs_ready"), S("ks_ready"), S("stored")

    with nc.Block() as block:
        @block.sync
        def _(sp):
            sp.dma_start(wqkv[:], k.dram["wqkv7"]).then_inc(loaded, 16)
            with sp.Fori(0, B) as b:
                sp.wait_ge(qs_ready, b + 1)
                sp.dma_start(q_parts[:, :, bass.ds(b * T, T)], qs[:]).then_inc(stored, 16)
                sp.wait_ge(ks_ready, b + 1)
                sp.dma_start(k_parts[:, :, bass.ds(b * T, T)], ks[:]).then_inc(stored, 16)
            sp.wait_ge(stored, 32 * B)

        @block.gpsimd
        def _(pool):
            nc.gpsimd.memset(v1[:], 1.0).then_inc(ones_ready, 1)
            with pool.Fori(0, B) as b:
                norm.pool(pool, b)

        @block.vector
        def _(dve):
            link = Chain(dve, chain)
            v = nc.vector
            dve.wait_ge(ones_ready, 1)
            with dve.Fori(0, B) as b:
                link.restart()
                norm.vector(dve, link, b, x, norm.xT_in_psum)
                dve.wait_ge(v_in_psum, b + 1)
                row = J * H * (HD + 1)
                v.tensor_copy(v1[:, bass.ds(b * row, row)].rearrange("p (h r c) -> p h r c", r=J, c=HD + 1)[:, :, :, 0:HD],
                              ps[:, 6 * BANK:8 * BANK].rearrange("p (r h c) -> p h r c", h=H, c=HD)).then_inc(v_ready, 1)
                dve.wait_ge(qT_ready, b + 1)
                dve.wait_ge(stored, 32 * b)
                split_rows(nc, k, link, qT[:], qs, D).then_inc(qs_ready, 1)
                dve.wait_ge(kT_ready, b + 1)
                split_rows(nc, k, link, kT[:], ks, D).then_inc(ks_ready, 1)

        @block.scalar
        def _(act):
            with act.Fori(0, B) as b:
                norm.scalar(act, b, v_in_psum)
                act.wait_ge(q_in_psum, b + 1)
                act.wait_ge(ks_ready, b)
                nc.scalar.mul(qT[:], ps[:, 2 * BANK:4 * BANK], SCALE).then_inc(qT_ready, 1)
                nc.scalar.copy(kT[:], ps[:, 4 * BANK:6 * BANK]).then_inc(kT_ready, 1)

        @block.tensor
        def _(pe):
            mm = nc.tensor.matmul
            pe.wait_ge(loaded, 16)
            with pe.Fori(0, B) as b:
                norm.tensor(pe, b)
                pe.wait_ge(norm.xT_ready, b + 1)
                pe.wait_ge(kT_ready, b)
                for h in range(2):
                    c = slice(h * BANK, (h + 1) * BANK)
                    mm(ps[:, 2 * BANK:4 * BANK][:, c], wqkv[:, 0:D], norm.xT[:, c], start=True, stop=True)
                    last = mm(ps[:, 4 * BANK:6 * BANK][:, c], wqkv[:, D:2 * D], norm.xT[:, c], start=True, stop=True)
                last.then_inc(q_in_psum, 1)
                pe.wait_ge(v_ready, b)
                for r in range(J):
                    last = mm(ps[:, 6 * BANK + r * D:6 * BANK + (r + 1) * D], norm.xT[:, r * P:(r + 1) * P],
                              wqkv[:, 2 * D:3 * D], start=True, stop=True)
                last.then_inc(v_in_psum, 1)


def attend(nc, k, q_parts, k_parts, v1, sums, topk):
    ps = k.ps
    S = k.sem
    qh, kh = k.sb("qh", [P, 2, T], BF16), k.sb("kh", [P, 2, T], BF16)
    identb, later = k.sb("identb", [P, P], BF16), k.sb("later", [P, P], BF16)
    e = k.sb("e", [P, 2, T])
    pT = k.sb("pT", [P, T])
    negmax = k.sb("negmax", [P, 2])
    pairs = B * H
    loaded, parts_loaded, parts_used = S("loaded"), S("parts_loaded"), S("parts_used")
    scores_in_psum, negmax_ready, scores_read, e_ready = (S("scores_in_psum"), S("negmax_ready"), S("scores_read"),
                                                          S("e_ready"))
    pT_in_psum, pT_ready, sums_in_psum, sums_ready = S("pT_in_psum"), S("pT_ready"), S("sums_in_psum"), S("sums_ready")
    loads = [(identb[:], k.dram["identb"]), (later[:], k.dram["later"])]
    if topk:
        bias_q, bias_k = k.sb("bias_q", [KBIAS, H * P], BF16), k.sb("bias_k", [KBIAS, T], BF16)
        loads += [(bias_q[:], k.dram["bias_q"]), (bias_k[:], k.dram["bias_k"])]
        rest, erest = k.sb("rest", [P, 2, T]), k.sb("erest", [P, 2, T])
        best = k.sb("best", [P, 2, HD])
        chain, rest_ready, erest_ready, p_ready = S("chain"), S("rest_ready"), S("erest_ready"), S("p_ready")
    else:
        p_ready = e_ready
    kv_heads = NKV if topk else H
    span = lambda r: (r + 1) * P
    sp_bank = lambda r: 2 * (r % 2) * BANK

    with nc.Block() as block:
        @block.sync
        def _(sp):
            for to, of in loads:
                sp.dma_start(to, of).then_inc(loaded, 16)
            with sp.Fori(0, pairs + 1) as i:
                at = (i % pairs) // H * T
                h = i % H
                g = h // (H // kv_heads)
                sp.wait_ge(parts_loaded, 18 * 16 * i)
                sp.wait_ge(parts_used, i)
                for u in range(3):
                    for w in range(3):
                        row = (3 * u + w) * HD
                        sp.dma_start(qh[row:row + HD, bass.ds(i % 2, 1), :],
                                     q_parts[bass.ds(h * HD, HD), u:u + 1, bass.ds(at, T)]).then_inc(parts_loaded, 16)
                        sp.dma_start(kh[row:row + HD, bass.ds(i % 2, 1), :],
                                     k_parts[bass.ds(g * HD, HD), w:w + 1, bass.ds(at, T)]).then_inc(parts_loaded, 16)
            sp.wait_ge(parts_loaded, 18 * 16 * (pairs + 1))

        @block.tensor
        def _(pe):
            mm = nc.tensor.matmul
            pe.wait_ge(loaded, 16 * len(loads))
            pe.sem_inc(parts_used, 1)

            def scores(i, r, t):
                if not (isinstance(t, int) and t < 2):
                    pe.wait_ge(e_ready, t - 1)
                for c in range(0, span(r), BANK):
                    n = min(BANK, span(r) - c)
                    to = ps[:, sp_bank(r) + c:sp_bank(r) + c + n]
                    diagonal = c + n == span(r)
                    mm(to, qh[0:KSPLIT, bass.ds(i % 2, 1), r * P:(r + 1) * P].rearrange("k o p -> k (o p)"),
                       kh[0:KSPLIT, bass.ds(i % 2, 1), c:c + n].rearrange("k o p -> k (o p)"), start=True,
                       stop=True)
                    if topk:
                        from_ = T - P - r * P + c
                        last = mm(to, bias_q[:, bass.ds(i % H * P, P)], bias_k[:, from_:from_ + n], start=False, stop=True,
                                  skip_group_check=True)
                    if diagonal:
                        last = mm(to[:, n - P:n], identb[:], later[:], start=False, stop=True, skip_group_check=True)
                last.then_inc(scores_in_psum, 1)

            def weigh(i, r):
                t = i * J + r
                pe.wait_ge(p_ready, t + 1)
                pe.wait_ge(pT_ready, 2 * t)
                for half in range(0, r + 1, 4):
                    for c in range(half, min(half + 4, r + 1)):
                        last = nc.tensor.transpose(ps[:, 4 * BANK + c * P:4 * BANK + (c + 1) * P],
                                                   e[:, r % 2, c * P:(c + 1) * P], k.ident[:])
                    last.then_inc(pT_in_psum, 1 if r >= 4 else 2)
                pe.wait_ge(sums_ready, t)
                g = (i % H) // (H // kv_heads)
                at = i // H * (J * kv_heads * (HD + 1)) + g * (HD + 1)
                for c in range(r + 1):
                    if c == 0:
                        pe.wait_ge(pT_ready, 2 * t + 1)
                    if c == 4 or r < 4 and c == 0:
                        pe.wait_ge(pT_ready, 2 * t + 2)
                    last = mm(ps[:, 6 * BANK:6 * BANK + HD + 1], pT[:, c * P:(c + 1) * P],
                              v1[:, bass.ds(at + c * kv_heads * (HD + 1), HD + 1)], start=(c == 0), stop=(c == r))
                last.then_inc(sums_in_psum, 1)

            pe.wait_ge(parts_loaded, 18 * 16)
            scores(0, 0, 0)
            scores(0, 1, 1)
            with pe.Fori(0, pairs) as i:
                for r in range(J):
                    if r < J - 2:
                        scores(i, r + 2, i * J + r + 2)
                    else:
                        if r == J - 2:
                            pe.wait_ge(parts_loaded, 18 * 16 * (i + 2))
                        scores(i + 1, r + 2 - J, (i + 1) * J + r + 2 - J)
                    if r == J - 3:
                        pe.wait_ge(scores_in_psum, (i + 1) * J)
                        pe.sem_inc(parts_used, 1)
                    weigh(i, r)

        @block.vector
        def _(dve):
            v = nc.vector
            if topk:
                link = Chain(dve, chain)
            with dve.Fori(0, pairs) as i:
                if topk:
                    link.restart()
                for r in range(J):
                    n, t, s = span(r), i * J + r, r % 2
                    scores_ = ps[:, sp_bank(r):sp_bank(r) + n]
                    dve.wait_ge(scores_in_psum, t + 1)
                    if not topk:
                        v.tensor_reduce(negmax[:, s:s + 1], scores_, AX.X, ALU.max, negate=True).then_inc(negmax_ready, 1)
                        continue
                    dve.wait_ge(erest_ready, t - 1 if r else t)
                    link(v.memset(best[:, s, :], NEG))
                    link(v.max(best[:, s, :], scores_))
                    v.tensor_scalar(negmax[:, s:s + 1], best[:, s, 0:1], -1.0, None, ALU.mult).then_inc(negmax_ready, 1)
                    for turn in range(TOPK // 8):
                        if turn:
                            link(v.max(best[:, s, :], rest[:, s, 0:n]))
                        ins = v.match_replace(rest[:, s, 0:n], best[:, s, :], rest[:, s, 0:n] if turn else scores_, NEG)
                        if turn == 0:
                            ins.then_inc(scores_read, 1)
                            link.settled()
                            dve.wait_ge(scores_read, t + 1)
                        elif turn == TOPK // 8 - 1:
                            ins.then_inc(rest_ready, 1)
                        else:
                            link(ins)

        @block.scalar
        def _(act):
            def copy_weights(i, r):
                t = i * J + r
                for half in range(2 if r >= 4 else 1):
                    act.wait_ge(pT_in_psum, 2 * t + 1 + half if r >= 4 else 2 * t + 2)
                    if half == 0:
                        act.wait_ge(sums_in_psum, t)
                    a, z = half * BANK, min(span(r), (half + 1) * BANK)
                    nc.scalar.copy(pT[:, a:z], ps[:, 4 * BANK + a:4 * BANK + z]).then_inc(pT_ready, 1 if r >= 4 else 2)
                act.wait_ge(sums_in_psum, t + 1)
                nc.scalar.copy(sums[:, bass.ds((i * J + r) * (HD + 1), HD + 1)], ps[:, 6 * BANK:6 * BANK + HD + 1]).then_inc(sums_ready, 1)

            with act.Fori(0, pairs) as i:
                for r in range(J):
                    n, t, s = span(r), i * J + r, r % 2
                    act.wait_ge(negmax_ready, t + 1)
                    if topk:
                        act.wait_ge(scores_read, t + 1)
                    nc.scalar.activation(e[:, s, 0:n], ps[:, sp_bank(r):sp_bank(r) + n], ACT.Exp,
                                         bias=negmax[:, s:s + 1]).then_inc(e_ready, 1)
                    if topk:
                        act.wait_ge(rest_ready, t + 1)
                        nc.scalar.activation(erest[:, s, 0:n], rest[:, s, 0:n], ACT.Exp,
                                             bias=negmax[:, s:s + 1]).then_inc(erest_ready, 1)
                    copy_weights(i, r)

        @block.gpsimd
        def _(pool):
            if topk:
                with pool.Fori(0, pairs) as i:
                    for r in range(J):
                        n, t, s = span(r), i * J + r, r % 2
                        pool.wait_ge(e_ready, t + 1)
                        pool.wait_ge(erest_ready, t + 1)
                        nc.gpsimd.tensor_tensor(e[:, s, 0:n], e[:, s, 0:n], erest[:, s, 0:n], ALU.subtract).then_inc(p_ready, 1)


HALVES = [(r, c, min(c + 4, r + 1)) for r in range(J) for c in range(0, r + 1, 4)]
BEFORE = [sum(1 for h in HALVES if h[0] < r) for r in range(J + 1)]
PAIRS = B * H
SUMS = J * (HD + 1)


def even_before(n):
    return (n + 1) // 2


class Weigh:

    def __init__(self, k, ps, v1, sums, p):
        self.nc, self.ps, self.v1, self.sums, self.p, self.ident = k.nc, ps, v1, sums, p, k.ident
        self.pT = k.sb("pT", [P, 2, T])
        self.v_now, self.v_last = k.sb("v_now", [P, SUMS]), k.sb("v_last", [P, SUMS])
        self.zeros = k.zeros
        self.v_next = k.sb("v_next", [P, SUMS])
        self.accT = k.sb("accT", [HD + 1, T])
        self.cleared, self.v_now_ready, self.v_last_ready = k.sem("cleared"), k.sem("v_now_ready"), k.sem("v_last_ready")
        self.transposed = k.sem("transposed")
        self.even_back, self.odd_back = k.sem("even_back"), k.sem("odd_back")
        self.weighed = k.sem("weighed")
        self.acc_copied, self.acc_transposed, self.stored = k.sem("acc_copied"), k.sem("acc_transposed"), k.sem("stored")

    def clear(self):
        g = self.nc.gpsimd
        g.memset(self.pT[:], 0.0).then_inc(self.cleared, 1)
        g.memset(self.v_last[:], 0.0).then_inc(self.cleared, 1)
        g.memset(self.accT[:], 0.0).then_inc(self.cleared, 1)

    def fetch_v(self, pool, link, i, kv_of_pair):
        g = self.nc.gpsimd
        link(g.tensor_copy(self.v_next[:], self.v1[:, bass.ds(kv_of_pair, SUMS)]))
        pool.wait_ge(self.weighed, i * J)
        g.tensor_tensor(self.v_now[:], self.v_next[:], self.zeros[:, 0:SUMS], ALU.add).then_inc(self.v_now_ready, 1)
        pool.wait_ge(self.weighed, i * J + 1)
        link(g.tensor_tensor(self.v_last[:], self.v_next[:], self.zeros[:, 0:SUMS], ALU.add))
        pool.sem_inc(self.v_last_ready, 1)

    def transpose(self, pe, i, r):
        for n, (_, c0, c1) in [(n, h) for n, h in enumerate(HALVES) if h[0] == r]:
            back = self.odd_back if n % 2 else self.even_back
            pe.wait_ge(back, i * (len(HALVES) // 2) + n // 2)
            at = (4 + n % 2) * BANK
            for c in range(c0, c1):
                last = self.nc.tensor.transpose(self.ps[:, at + (c - c0) * P:at + (c - c0 + 1) * P],
                                                self.p[:, r % 2, c * P:(c + 1) * P], self.ident[:])
            last.then_inc(self.transposed, 1)

    def multiply(self, pe, i, r):
        n = BEFORE[r + 1]
        pe.wait_ge(self.even_back, i * (len(HALVES) // 2) + even_before(n))
        pe.wait_ge(self.odd_back, i * (len(HALVES) // 2) + n - even_before(n))
        if r == 0:
            pe.wait_ge(self.acc_copied, i + 1)
            pe.wait_ge(self.v_now_ready, i + 1)
        if r == -1:
            pe.wait_ge(self.v_last_ready, i)
        r, v = (r, self.v_now) if r >= 0 else (J - 1, self.v_last)
        to = self.ps[0:HD + 1, 6 * BANK + r * P:6 * BANK + (r + 1) * P]
        for c in range(r + 1):
            last = self.nc.tensor.matmul(to, v[:, c * (HD + 1):(c + 1) * (HD + 1)], self.pT[:, r % 2, c * P:(c + 1) * P],
                                         start=(c == 0), stop=(c == r))
        last.then_inc(self.weighed, 1)

    def bring_back(self, eng, i, r, odd):
        for n, (_, c0, c1) in [(n, h) for n, h in enumerate(HALVES) if h[0] == r and h[1] >= 0]:
            if n % 2 != odd:
                continue
            eng.wait_ge(self.transposed, i * len(HALVES) + n + 1)
            eng.wait_ge(self.weighed, i * J + r)
            at = (4 + odd) * BANK
            of, to = self.ps[:, at:at + (c1 - c0) * P], self.pT[:, r % 2, c0 * P:c1 * P]
            if odd:
                self.nc.scalar.copy(to, of).then_inc(self.odd_back, 1)
            else:
                self.nc.vector.tensor_copy(to, of).then_inc(self.even_back, 1)

    def copy_acc(self, act, i):
        act.wait_ge(self.weighed, i * J + 1)
        self.nc.scalar.copy(self.accT[:], self.ps[0:HD + 1, 6 * BANK:8 * BANK]).then_inc(self.acc_copied, 1)

    def transpose_acc(self, pe, i):
        for r in range(J):
            at = 3 * BANK + r * (HD + 1)
            last = self.nc.tensor.transpose(self.ps[:, at:at + HD + 1], self.accT[:, r * P:(r + 1) * P],
                                            self.ident[0:HD + 1, 0:HD + 1])
        last.then_inc(self.acc_transposed, 1)

    def store(self, act, i):
        act.wait_ge(self.acc_transposed, i + 1)
        self.nc.scalar.copy(self.sums[:, bass.ds(i * SUMS, SUMS)], self.ps[:, 3 * BANK:3 * BANK + SUMS]).then_inc(self.stored, 1)


def attend_causal(nc, k, q_parts, k_parts, v1, sums):
    ps = k.ps
    S = k.sem
    qh, kh = k.sb("qh", [P, 2, T], BF16), k.sb("kh", [P, 2, T], BF16)
    identb, later = k.sb("identb", [P, P], BF16), k.sb("later", [P, P], BF16)
    e = k.sb("e", [P, 2, T])
    negmax = k.sb("negmax", [P, 2])
    loaded, parts_loaded, scores_in_psum = S("loaded"), S("parts_loaded"), S("scores_in_psum")
    negmax_ready, e_ready, fetched = S("negmax_ready"), S("e_ready"), S("fetched")
    weigh = Weigh(k, ps, v1, sums, e)
    loads = [(identb[:], k.dram["identb"]), (later[:], k.dram["later"])]
    span = lambda r: (r + 1) * P
    bank_of = lambda r: 2 * (r % 2) * BANK

    with nc.Block() as block:
        @block.sync
        def _(sp):
            for to, of in loads:
                sp.dma_start(to, of).then_inc(loaded, 16)
            load_parts(sp, 0, H, qh, kh, q_parts, k_parts, parts_loaded)
            with sp.Fori(1, PAIRS + 1) as i:
                sp.wait_ge(parts_loaded, 18 * 16 * i)
                sp.wait_ge(scores_in_psum, i * J - J)
                load_parts(sp, i, H, qh, kh, q_parts, k_parts, parts_loaded)
            sp.wait_ge(parts_loaded, 18 * 16 * (PAIRS + 1))

        @block.gpsimd
        def _(pool):
            weigh.clear()
            pool.wait_ge(weigh.cleared, 3)
            link = Chain(pool, fetched)
            with pool.Fori(0, PAIRS) as i:
                link.restart()
                weigh.fetch_v(pool, link, i, i * SUMS)

        @block.tensor
        def _(pe):
            mm = nc.tensor.matmul

            def scores(i, r):
                for c in range(0, span(r), BANK):
                    n = min(BANK, span(r) - c)
                    to = ps[:, bank_of(r) + c:bank_of(r) + c + n]
                    last = mm(to, qh[0:KSPLIT, bass.ds(i % 2, 1), r * P:(r + 1) * P].rearrange("k o p -> k (o p)"),
                              kh[0:KSPLIT, bass.ds(i % 2, 1), c:c + n].rearrange("k o p -> k (o p)"), start=True, stop=True)
                    if c + n == span(r):
                        last = mm(to[:, n - P:n], identb[:], later[:], start=False, stop=True, skip_group_check=True)
                last.then_inc(scores_in_psum, 1)

            pe.wait_ge(loaded, 16 * len(loads))
            pe.wait_ge(weigh.cleared, 3)
            pe.wait_ge(parts_loaded, 18 * 16)
            scores(0, 0)
            scores(0, 1)
            with pe.Fori(0, PAIRS) as i:
                for r in range(J):
                    pe.wait_ge(e_ready, i * J + r + 1)
                    if r == 3:
                        pe.wait_ge(weigh.stored, i + 1)
                    if r == J - 2:
                        pe.wait_ge(parts_loaded, 18 * 16 * (i + 2))
                    scores(*((i, r + 2) if r < J - 2 else (i + 1, r + 2 - J)))
                    weigh.transpose(pe, i, r)
                    weigh.multiply(pe, i, r - 1)
                    if r == 1:
                        weigh.transpose_acc(pe, i)
            weigh.multiply(pe, PAIRS, -1)
            pe.wait_ge(weigh.acc_copied, PAIRS + 1)
            weigh.transpose_acc(pe, PAIRS)

        @block.vector
        def _(dve):
            def maximum(r, t):
                dve.wait_ge(scores_in_psum, t + 1)
                if not isinstance(t, int):
                    dve.wait_ge(e_ready, t - 1)
                nc.vector.tensor_reduce(negmax[:, r % 2:r % 2 + 1], ps[:, bank_of(r):bank_of(r) + span(r)], AX.X, ALU.max,
                                        negate=True).then_inc(negmax_ready, 1)

            maximum(0, 0)
            with dve.Fori(0, PAIRS) as i:
                for r in range(J):
                    maximum((r + 1) % J, i * J + r + 1)
                    weigh.bring_back(dve, i, r, 0)

        @block.scalar
        def _(act):
            def exp(r, t, used):
                act.wait_ge(negmax_ready, t + 1)
                if used is not None:
                    act.wait_ge(weigh.transposed, used)
                nc.scalar.activation(e[:, r % 2, 0:span(r)], ps[:, bank_of(r):bank_of(r) + span(r)], ACT.Exp,
                                     bias=negmax[:, r % 2:r % 2 + 1]).then_inc(e_ready, 1)

            exp(0, 0, None)
            with act.Fori(0, PAIRS) as i:
                for r in range(J):
                    exp((r + 1) % J, i * J + r + 1, i * len(HALVES) + BEFORE[r])
                    if r == 2:
                        weigh.store(act, i)
                    weigh.bring_back(act, i, r, 1)
                    if r == 0:
                        weigh.copy_acc(act, i)
            weigh.copy_acc(act, PAIRS)
            weigh.store(act, PAIRS)


def load_parts(sp, i, kv_heads, qh, kh, q_parts, k_parts, parts_loaded):
    at = (i % PAIRS) // H * T
    h = i % H
    g = h // (H // kv_heads)
    for u in range(3):
        for w in range(3):
            row = (3 * u + w) * HD
            sp.dma_start(qh[row:row + HD, bass.ds(i % 2, 1), :],
                         q_parts[bass.ds(h * HD, HD), u:u + 1, bass.ds(at, T)]).then_inc(parts_loaded, 16)
            sp.dma_start(kh[row:row + HD, bass.ds(i % 2, 1), :],
                         k_parts[bass.ds(g * HD, HD), w:w + 1, bass.ds(at, T)]).then_inc(parts_loaded, 16)



def topk_attention(nc, k, x):
    v1 = k.sb("v1", [P, B * J * NKV * (HD + 1)])
    stages = k.ctx
    with ExitStack() as k.ctx:
        project_topk(nc, k, x, k.q_parts, k.k_parts, v1)
    k.ctx = stages
    sums = k.sb("sums", [P, B * H * J * (HD + 1)])
    with ExitStack() as k.ctx:
        attend(nc, k, k.q_parts, k.k_parts, v1, sums, topk=True)
    k.ctx = stages
    ps = k.ps
    S = k.sem
    wo, bo = k.sb("wo", [D, D]), k.sb("bo", [P, D])
    inverse, y, yT = k.sb("inverse", [P, H * J]), k.sb("y", [P, J, H, HD]), k.sb("yT", [D, T])
    loaded, chain, y_ready, yT_in_psum, yT_ready = S("loaded"), S("chain"), S("y_ready"), S("yT_in_psum"), S("yT_ready")
    out_in_psum, x_updated = S("out_in_psum"), S("x_updated")

    with nc.Block() as block:
        @block.sync
        def _(sp):
            sp.dma_start(wo[:], k.dram["wo5"]).then_inc(loaded, 16)
            sp.dma_start(bo[:], k.dram["bo5"].partition_broadcast(P)).then_inc(loaded, 16)

        @block.vector
        def _(dve):
            link = Chain(dve, chain)
            v = nc.vector
            dve.wait_ge(loaded, 32)
            with dve.Fori(0, B) as b:
                link.restart()
                mine = H * J * (HD + 1)
                got = sums[:, bass.ds(b * mine, mine)].rearrange("p (h r c) -> p h r c", h=H, r=J)
                link(v.reciprocal(inverse[:].rearrange("p (h r) -> p h r", h=H), got[:, :, :, HD]))
                v.tensor_tensor(y[:].rearrange("p r h c -> p h r c"), got[:, :, :, 0:HD],
                                inverse[:].rearrange("p (h r) -> p h r", h=H).unsqueeze(3).broadcast_to([P, H, J, HD]),
                                ALU.mult).then_inc(y_ready, 1)
                link(v.tensor_tensor(jd(rows_of(x, b)), jd(rows_of(x, b)), middle(bo[:], J), ALU.add))
                dve.wait_ge(out_in_psum, b + 1)
                v.tensor_tensor(rows_of(x, b), rows_of(x, b), ps[:, 2 * BANK:4 * BANK], ALU.add).then_inc(x_updated, 1)

        @block.scalar
        def _(act):
            with act.Fori(0, B) as b:
                act.wait_ge(yT_in_psum, b + 1)
                nc.scalar.copy(yT[:], ps[:, 0:2 * BANK]).then_inc(yT_ready, 1)

        @block.tensor
        def _(pe):
            pe.wait_ge(loaded, 32)
            with pe.Fori(0, B) as b:
                pe.wait_ge(y_ready, b + 1)
                for r in range(J):
                    last = nc.tensor.transpose(ps[:, r * P:(r + 1) * P], y[:, r].rearrange("p h c -> p (h c)"), k.ident[:])
                last.then_inc(yT_in_psum, 1)
                pe.wait_ge(yT_ready, b + 1)
                pe.wait_ge(x_updated, b)
                for j in range(J):
                    at = 2 * BANK + j * D
                    last = nc.tensor.matmul(ps[:, at:at + D], by_token(yT[:])[:, j, :], wo[:], start=True, stop=True)
                last.then_inc(out_in_psum, 1)


def causal_attention(nc, k, x):
    v1 = k.sb("v1", [P, B * J * H * (HD + 1)])
    stages = k.ctx
    with ExitStack() as k.ctx:
        project_causal(nc, k, x, k.q_parts, k.k_parts, v1)
    k.ctx = stages
    sums = k.sb("sums", [P, (PAIRS + 1) * SUMS])
    with ExitStack() as k.ctx:
        attend_causal(nc, k, k.q_parts, k.k_parts, v1, sums)
    k.ctx = stages
    ps = k.ps
    S = k.sem
    wo, ones = k.sb("wo", [P, D]), k.sb("ones", [P, P])
    wsum, factor, y = k.sb("wsum", [P, D]), k.sb("factor", [P, D]), k.sb("y", [P, J, D])
    loaded, ones_ready, wsum_in_psum, chain = S("loaded"), S("ones_ready"), S("wsum_in_psum"), S("chain")

    with nc.Block() as block:
        @block.sync
        def _(sp):
            sp.dma_start(wo[:], k.dram["wo7"]).then_inc(loaded, 16)

        @block.gpsimd
        def _(pool):
            nc.gpsimd.memset(ones[:], 1.0).then_inc(ones_ready, 1)

        @block.tensor
        def _(pe):
            pe.wait_ge(loaded, 16)
            pe.wait_ge(ones_ready, 1)
            nc.tensor.matmul(ps[:, 0:D], ones[:], wo[:], start=True, stop=True).then_inc(wsum_in_psum, 1)

        @block.vector
        def _(dve):
            link = Chain(dve, chain)
            v = nc.vector
            dve.wait_ge(wsum_in_psum, 1)
            link(v.tensor_copy(wsum[:], ps[:, 0:D]))
            with dve.Fori(0, B) as b:
                link.restart()
                mine = D * (HD + 1)
                got = sums[:, bass.ds(b * mine + SUMS, mine)].rearrange("p (d c) -> p c d", c=HD + 1)
                link(v.reciprocal(factor[:], got[:, HD, :]))
                link(v.tensor_tensor(factor[:], factor[:], wsum[:], ALU.mult))
                link(v.tensor_tensor(y[:], got[:, 0:HD, :], middle(factor[:], J), ALU.mult))
                link(v.tensor_tensor(jd(rows_of(x, b)), jd(rows_of(x, b)), y[:], ALU.add))


STAGES = [linear_attention, fp4_ffn, mamba, fp4_ffn, topk_attention, low_rank_ffn, causal_attention, low_rank_ffn]


def build(nc, dram, out, n_stages=None):
    with ExitStack() as ctx:
        k = Kernel(nc, dram, ctx)
        x = k.sb("x", [P, B * T])
        k.ps = ctx.enter_context(nc.psum_tensor("banks", [P, 8 * BANK], F32))
        k.ident = k.sb("ident", [P, P])
        k.minus_half = k.sb("minus_half", [P, J * 20])
        k.zeros = k.sb("zeros", [P, P])
        k.q_parts = nc.dram_tensor("q_parts", (D, 3, B * T), BF16, kind="Internal").ap()
        k.k_parts = nc.dram_tensor("k_parts", (D, 3, B * T), BF16, kind="Internal").ap()
        k.wgateT, k.wupT = k.sb("wgateT", [D, FF4]), k.sb("wupT", [D, FF4])
        k.wdownT = k.sb("wdownT", [P, 3 * D])
        load(nc, k, x, [(k.ident[:], dram["ident"])])
        with ExitStack() as inner:
            k.ctx = inner
            fp4_weights(nc, k, x)
        k.end_stage()
        for stage in STAGES[:n_stages]:
            with ExitStack() as inner:
                k.ctx = inner
                stage(nc, k, x)
            k.end_stage()
        k.ctx = ctx
        store(nc, k, x, out)


def constants():
    c = {"ident": np.eye(P, dtype=np.float32)}
    inv = 1.0 / 500000.0 ** (np.arange(0, HD, 2, dtype=np.float32) / np.float32(HD))
    f = np.arange(T, dtype=np.float32)[:, None] * inv.astype(np.float32)[None, :]
    emb = np.concatenate([f, f], axis=-1)
    sign = np.where(np.arange(HD) < HD // 2, -1.0, 1.0).astype(np.float32)
    cos, sin = np.cos(emb).astype(np.float32), (np.sin(emb) * sign).astype(np.float32)
    cos, sin = np.tile(cos, (1, H)), np.tile(sin, (1, H))
    c["cosT"], c["sinT"] = cos.T.copy(), sin.T.copy()
    blocks = lambda a: a.reshape(J, P, D).transpose(1, 0, 2).reshape(P, T).copy()
    c["cos"], c["sin"] = blocks(cos), blocks(sin)
    c["same_head"] = np.kron(np.eye(H), np.ones((HD, HD))).astype(np.float32)
    bf16 = mybir.dt.np(BF16)
    rows = np.arange(3 * 2 * NS) % (2 * NS)
    pick = (rows[:, None] == np.arange(2 * NS)[None, :]).astype(np.float32)
    c["pick"] = np.repeat(pick[:, :, None], P, 2).astype(bf16)
    c["identb"] = np.eye(P).astype(bf16)
    c["later"] = np.where(np.arange(P)[None, :] > np.arange(P)[:, None], NEG, 0.0).astype(bf16)

    def parts(a):
        got = []
        for _ in range(3):
            got.append(a.astype(bf16))
            a = a - got[-1].astype(np.float32)
        return got

    slopes = (2.0 ** -(np.arange(H, dtype=np.float32) / (H - 1) * 8.0)).astype(np.float32)
    per_query = [np.repeat(a, P) for a in parts(slopes)]
    down = parts(-(slopes[:, None] * np.arange(P, dtype=np.float32)).reshape(-1))
    c["bias_q"] = np.stack(per_query * 2 + down)
    offset = np.arange(T) - (T - P)
    low = offset % 8
    one = np.ones(T)
    c["bias_k"] = np.stack([offset - low] * 3 + [low] * 3 + [one] * 3).astype(bf16)
    return c


def layout(inputs):
    a = {n: np.asarray(v) for n, v in inputs.items()}
    m = constants()
    m["x"] = a["L0_attn_a_x"]
    w = a["L0_attn_a_W_qkv"]
    half = lambda w: w.reshape(D, H, 2, HD // 2)[:, :, ::-1].reshape(D, D)
    m["wq0"] = np.concatenate([w[:, 0:D], half(w[:, 0:D])], 1)
    m["wkv0"] = np.concatenate([w[:, D:2 * D], half(w[:, D:2 * D]), w[:, 2 * D:]], 1)
    m["wout0"] = a["L0_attn_a_W_out"]
    m["win"], m["wout3"] = a["L0_attn_b_W_in"].T, a["L0_attn_b_W_out"].T
    wx = a["L0_attn_b_W_x"].T
    m["wx"] = np.concatenate([wx[:, 0:E_IN]] + 3 * [wx[:, E_IN:]], 1)
    m["cw"], m["cb"] = a["L0_attn_b_conv_w"][:, 0, :], a["L0_attn_b_conv_b"]
    m["skip"], m["alog"] = a["L0_attn_b_D"], a["L0_attn_b_A_log"]
    m["wqkv5"] = np.concatenate([a["L1_attn_a_wq"], a["L1_attn_a_wkv"]], 1)
    m["bqkv5"] = np.concatenate([a["L1_attn_a_bq"], a["L1_attn_a_bkv"]])
    m["gain5"] = np.concatenate([np.tile(a["L1_attn_a_qn_w"], H), np.tile(a["L1_attn_a_kn_w"], NKV)])
    m["wo5"], m["bo5"] = a["L1_attn_a_wo"], a["L1_attn_a_bo"]
    m["wqkv7"] = a["L1_attn_b_W_qkv"].reshape(H, D, 3, HD).transpose(1, 2, 0, 3).reshape(D, 3 * D)
    m["wo7"] = a["L1_attn_b_W_out"].reshape(H * HD, D)
    m["wgate"], m["wup"], m["wdown"] = a["L0_ffn_w_gate"], a["L0_ffn_w_up"], a["L0_ffn_w_down"]
    m["u1"], m["v1"], m["b1"], m["u2"] = a["L1_ffn_U1"], a["L1_ffn_V1"], a["L1_ffn_b1"], a["L1_ffn_U2"]
    m["v2"] = np.concatenate([a["L1_ffn_V2"], a["L1_ffn_b2"][None]], 0)
    return {n: np.ascontiguousarray(v) for n, v in m.items()}


def kernel(**inputs):
    import concourse.bacc as bacc
    from concourse.bass_utils import run_bass_kernel_spmd

    arrays = layout(inputs)
    nc = bacc.Bacc("TRN2", target_bir_lowering=False, num_devices=1)
    dram = {n: nc.dram_tensor(f"in_{n}", v.shape, mybir.dt.from_np(v.dtype), kind="ExternalInput").ap()
            for n, v in arrays.items()}
    out = nc.dram_tensor("out", (B, T, D), F32, kind="ExternalOutput").ap()
    build(nc, dram, out)
    r = run_bass_kernel_spmd(nc, [{f"in_{n}": v for n, v in arrays.items()}], core_ids=[0])
    return r.results[0]["out"]
```
